# Optimizing a Trainium2 kernel written in Bass

```python
import numpy as np
import jax
import jax.numpy as jnp

def _softmax(x, axis=-1):
    return jax.nn.softmax(x, axis=axis)

def _gelu(x):
    return jax.nn.gelu(x, approximate=True)

def _silu(x):
    return jax.nn.silu(x)

def _sigmoid(x):
    return jax.nn.sigmoid(x)

def _layernorm(x, axis=-1, eps=1e-05):
    m = jnp.mean(x, axis=axis, keepdims=True)
    v = jnp.var(x, axis=axis, keepdims=True)
    return (x - m) / jnp.sqrt(v + eps)

def _scatter_add(tgt, idx, src, axis=0):
    return tgt.at[idx].add(src)

def _segment_sum(src, seg, n):
    return jax.ops.segment_sum(src, seg, n)
kernel_name = 'mk_decoder_postln_d1_seqx_r4_d40838'

def setup_inputs(seed: int=0):
    np.random.seed(seed)
    _w = jnp.asarray

    def _rec_inputs():
        import jax
        import jax.numpy as jnp
        _rk = jax.random.key(seed)
        x = -0.0003929 + 0.9999 * jax.random.normal(jax.random.fold_in(_rk, 1), (16, 128, 256), jnp.float32)
        _lenS = 128 - jax.random.randint(jax.random.fold_in(_rk, 7), (16,), 0, max(1, 128 // 4) + 1, jnp.int32)
        _lenS2 = 128 - jax.random.randint(jax.random.fold_in(_rk, 8), (16,), 0, max(1, 128 // 4) + 1, jnp.int32)
        _ctx_1024P = jax.random.normal(jax.random.fold_in(_rk, 11), (16, 16, 256), jnp.float32)
        _ctx_1024c = jax.random.dirichlet(jax.random.fold_in(_rk, 511), 0.3 * jnp.ones((16,), jnp.float32), (16, 128))
        _ctx_1024t = jnp.einsum('bsk,bkd->bsd', _ctx_1024c, _ctx_1024P)
        _ctx_1024t = _ctx_1024t * jax.lax.rsqrt(jnp.mean(jnp.square(_ctx_1024t)) + 1e-12) * 0.953939
        ctx_1024 = 2.81802e-05 + 1.00001 * (_ctx_1024t + 0.3 * jax.random.normal(jax.random.fold_in(_rk, 611), (16, 128, 256), jnp.float32))
        return (x, ctx_1024)
    x, ctx_1024 = _rec_inputs()

    def _L0_attn_setup():
        import jax, jax.numpy as jnp
        import numpy as np
        TWO_PI = 6.283185307179586
        key = jax.random.key(seed)
        k1, k2, k3, k4, k5, k6 = jax.random.split(key, 6)
        B, T, D = (2, 2048, 256)
        x = jax.random.normal(k1, (B, T, D), dtype=jnp.float32)
        s = 1.0 / np.sqrt(D)
        Wk = jax.random.uniform(k2, (D, D), jnp.float32, -s, s)
        Wv = jax.random.uniform(k3, (D, D), jnp.float32, -s, s)
        Wo = jax.random.uniform(k4, (D, D), jnp.float32, -s, s)
        freqs = jax.random.uniform(k5, (D,), jnp.float32, 0.0, TWO_PI)
        return {'x': x, 'Wk': Wk, 'Wv': Wv, 'Wo': Wo, 'freqs': freqs}
    _L0_attn_all = _L0_attn_setup()
    _L0_attn_in = {k: v for k, v in _L0_attn_all.items() if k in ('Wk', 'Wv', 'Wo', 'freqs')}
    del _L0_attn_all

    def _L0_xattn_setup():
        import jax, jax.numpy as jnp
        import numpy as np
        GAMMA = 0.96875

        def _decay_matrix(S):
            idx = jnp.arange(S, dtype=jnp.float32)
            dec = GAMMA ** (idx[:, None] - idx[None, :])
            return jnp.triu(dec).T
        key = jax.random.key(seed)
        kq, kk, kv = jax.random.split(key, 3)
        B, S, D = (8, 512, 256)
        Q = jax.random.normal(kq, (B, S, D), dtype=jnp.float32)
        K = jax.random.normal(kk, (B, S, D), dtype=jnp.float32)
        V = jax.random.normal(kv, (B, S, D), dtype=jnp.float32)
        return {'Q': Q, 'K': K, 'V': V}
    _L0_xattn_all = _L0_xattn_setup()
    _L0_xattn_in = {k: v for k, v in _L0_xattn_all.items() if k in ()}
    del _L0_xattn_all

    def _L0_ffn_setup():
        import jax, jax.numpy as jnp
        import numpy as np
        E = 8
        H = 256
        D = 256
        TOP_K = 2
        key = jax.random.key(seed)
        k0, k1, k2, k3 = jax.random.split(key, 4)
        x = jax.random.normal(k0, (1, 512, H), dtype=jnp.float32)
        router_w = jax.random.normal(k1, (E, H), dtype=jnp.float32) * (1.0 / np.sqrt(H))
        up_proj = jax.random.normal(k2, (E, H, 2 * D), dtype=jnp.float32) * (1.0 / np.sqrt(H))
        down_proj = jax.random.normal(k3, (E, D, H), dtype=jnp.float32) * (1.0 / np.sqrt(D))
        return {'x': x, 'router_w': router_w, 'up_proj': up_proj, 'down_proj': down_proj}
    _L0_ffn_all = _L0_ffn_setup()
    _L0_ffn_in = {k: v for k, v in _L0_ffn_all.items() if k in ('router_w', 'up_proj', 'down_proj')}
    del _L0_ffn_all
    return {'x': x, 'ctx_1024': ctx_1024, 'L0_attn_Wk': _L0_attn_in['Wk'], 'L0_attn_Wv': _L0_attn_in['Wv'], 'L0_attn_Wo': _L0_attn_in['Wo'], 'L0_attn_freqs': _L0_attn_in['freqs'], 'L0_ffn_router_w': _L0_ffn_in['router_w'], 'L0_ffn_up_proj': _L0_ffn_in['up_proj'], 'L0_ffn_down_proj': _L0_ffn_in['down_proj']}

def reference(x, ctx_1024, L0_attn_Wk, L0_attn_Wv, L0_attn_Wo, L0_attn_freqs, L0_ffn_router_w, L0_ffn_up_proj, L0_ffn_down_proj):
    import jax
    import jax.numpy as jnp

    def _L0_attn_ref(x, Wk, Wv, Wo, freqs):
        import jax, jax.numpy as jnp
        import numpy as np
        TWO_PI = 6.283185307179586
        B, T, C = x.shape
        k_real = x @ Wk.T
        v_real = x @ Wv.T
        v = v_real.astype(jnp.complex64)
        t = jnp.arange(T, dtype=jnp.float32)
        rotors = jnp.exp(1j * (t[:, None] * freqs[None, :])).astype(jnp.complex64)
        memory_trace = jnp.cumsum(v * rotors[None, :, :], axis=1)
        retrieved = jnp.real(memory_trace * jnp.conj(rotors)[None, :, :])
        return retrieved @ Wo.T

    def _L0_xattn_ref(Q, K, V):
        import jax, jax.numpy as jnp
        import numpy as np
        GAMMA = 0.96875

        def _decay_matrix(S):
            idx = jnp.arange(S, dtype=jnp.float32)
            dec = GAMMA ** (idx[:, None] - idx[None, :])
            return jnp.triu(dec).T
        B, S, d = Q.shape
        x = jnp.einsum('bsd,btd->bst', Q, K) / d ** 0.5
        Dm = _decay_matrix(S)
        Dm = Dm / jnp.sqrt(jnp.sum(Dm, axis=1))
        x = x * Dm
        v = jnp.maximum(jnp.abs(jnp.sum(x, axis=-1)), 1.0)
        x = x / v[:, None, :]
        return jnp.einsum('bst,btd->bsd', x, V)

    def _L0_ffn_ref(x, router_w, up_proj, down_proj):
        import jax, jax.numpy as jnp
        import numpy as np
        E = 8
        H = 256
        D = 256
        TOP_K = 2
        B, T, _ = x.shape
        xt = x.reshape(-1, H)
        N = xt.shape[0]
        logits = jnp.einsum('nh,eh->ne', xt, router_w)
        probs = jax.nn.softmax(logits, axis=-1)
        scores, expert_idx = jax.lax.top_k(probs, TOP_K)
        scores = scores / jnp.sum(scores, axis=-1, keepdims=True)
        gate = jnp.zeros((N, E), dtype=xt.dtype).at[jnp.arange(N)[:, None], expert_idx].add(scores)
        h = jnp.einsum('nh,ehd->end', xt, up_proj)
        hidden = jax.nn.silu(h[..., :D]) * h[..., D:]
        out_e = jnp.einsum('end,edh->enh', hidden, down_proj)
        out = jnp.einsum('ne,enh->nh', gate, out_e)
        return out.reshape(B, T, H)
    x = _layernorm(x + _L0_attn_ref(x, L0_attn_Wk, L0_attn_Wv, L0_attn_Wo, L0_attn_freqs), axis=-1)
    x = _layernorm(x + _L0_xattn_ref(x, ctx_1024, ctx_1024), axis=-1)
    x = _layernorm(x + _L0_ffn_ref(x, L0_ffn_router_w, L0_ffn_up_proj, L0_ffn_down_proj), axis=-1)
    return x

_drawn_inputs = setup_inputs


def setup_inputs(seed=0):
    import zlib

    import numpy as np

    out = dict(_drawn_inputs(seed))
    spreads = {}
    factors = {}
    for name, (base, spread) in spreads.items():
        noise = np.random.default_rng([zlib.crc32(name.encode()), seed]).standard_normal(out[name].shape)
        drawn = base * np.exp(spread * noise) if base else spread * noise
        out[name] = jnp.asarray(drawn.astype(out[name].dtype))
    for name, factor in factors.items():
        out[name] = (out[name] * factor).astype(out[name].dtype)
    return out
```

```python
from contextlib import ExitStack

import numpy as np

import concourse.bass as bass
from concourse import mybir

ALU = mybir.AluOpType
ACT = mybir.ActivationFunctionType
AX_X = mybir.AxisListType.X
F32 = mybir.dt.float32
F32R = mybir.dt.float32r
F16 = mybir.dt.float16
I32 = mybir.dt.int32

P = 128
B, T, D = 16, 128, 256
KC = D // P
PAIRS = B // 2
E, DH = 8, 256
TOPK = 2
N = B * T
TILES = (N * TOPK + E * (P - 1)) // P
EPS = 1e-5
GAMMA = 0.96875
SKIP = 4 * N

ROUND = 12582912.0
TWO_PI = 2.0 * np.pi
TURN_HI = 6.28125
TURN_MID = float(np.float32(np.round((TWO_PI - TURN_HI) * 2.0 ** 21) / 2.0 ** 21))
TURN_LO = float(np.float32(TWO_PI - TURN_HI - TURN_MID))
SIN_MAX = 3.1415925

C_DECAY, C_TRI, C_IDENT, C_ONE, C_TOK, C_ROW = 0, P, 2 * P, 3 * P, 3 * P + 1, 3 * P + 2
C_TOKID = C_ROW + P
C_PREF = C_TOKID + B
C_END = C_PREF + E
H_STRICT, H_ONES, H_ROW, H_END = 0, P, 2 * P, 3 * P
W_UP, W_DOWN = 0, KC * 2 * DH
W_END = W_DOWN + KC * D
RING = 3
HALF = 63.5


def shape_constants():
    i = np.arange(P)
    decay = np.where(i[:, None] >= i[None, :], GAMMA ** (i[None, :] - i[:, None]).astype(np.float64), 0.0)
    decay = decay / np.sqrt(decay.sum(1))[None, :] / np.sqrt(D)
    c = np.zeros((P, C_END), np.float32)
    c[:, C_DECAY:C_DECAY + P] = decay.T
    c[:, C_TRI:C_TRI + P] = i[:, None] <= i[None, :]
    c[:, C_IDENT:C_IDENT + P] = np.eye(P)
    c[:, C_ONE] = 1.0
    c[:, C_TOK] = i
    c[:, C_ROW:C_ROW + P] = i[None, :]
    c[:, C_TOKID:C_TOKID + B] = i[:, None] + P * np.arange(B)[None, :]
    c[:, C_PREF:C_PREF + E] = E - np.arange(E)[None, :]
    h = np.zeros((P, H_END), np.float16)
    h[:, H_STRICT:H_STRICT + P] = i[:, None] < i[None, :]
    h[:, H_ONES:H_ONES + P] = 1.0
    h[:, H_ROW:H_ROW + P] = i[None, :]
    return c, h


def decoder_block(nc, x, xT, ctxt, ctxT, wvT, woT, freq_row, freq_col, routerT, weights, consts, halves, out):
    with ExitStack() as scope:
        def sb(name, shape, dt=F32):
            return scope.enter_context(nc.sbuf_tensor(name, shape, dt))

        def ps(name, shape, dt=F32):
            return scope.enter_context(nc.psum_tensor(name, shape, dt))

        def sem(name):
            return scope.enter_context(nc.semaphore(name))

        const = sb("const", [P, C_END])
        wv = sb("wv", [P, KC, D])
        wo = sb("wo", [P, KC, D])
        wr = sb("wr", [P, KC, E])
        frow = sb("frow", [P, D])
        fcol = sb("fcol", [P, KC])
        angle = sb("angle", [P, 2, D])
        turns = sb("turns", [P, 2, D])
        rem = sb("rem", [P, 2, D])
        rotor = sb("rotor", [P, 2, 2, D])

        x_in = [sb(f"x_in{s}", [P, 2, D]) for s in range(2)]
        xT_in = [sb(f"xT_in{s}", [P, 2, KC, T]) for s in range(2)]
        c_in = [sb(f"c_in{s}", [P, 2, D]) for s in range(2)]
        cT_in = [sb(f"cT_in{s}", [P, 2, KC, T]) for s in range(2)]
        turned = sb("turned", [P, 2, 2, D])
        back = sb("back", [P, 2, 2, D])
        got = sb("got", [P, 2, KC, T])
        r1 = sb("r1", [P, 2, D])
        st1 = sb("st1", [P, 2, 6])
        mv1 = sb("mv1", [P, 2, 2])
        sd1 = sb("sd1", [P, 2])
        rs1 = sb("rs1", [P, 2])
        x1 = [sb(f"x1_{s}", [P, 2, D]) for s in range(2)]
        x1T = sb("x1T", [P, 2, KC, T])
        att = sb("att", [P, 2, T])
        vabs = sb("vabs", [P, 2])
        vmax = sb("vmax", [P, 2])
        vinv = sb("vinv", [P, 2])
        cs = sb("cs", [P, 2, D])
        r2 = sb("r2", [P, 2, D])
        st2 = sb("st2", [P, 2, 6])
        mv2 = sb("mv2", [P, 2, 2])
        sd2 = sb("sd2", [P, 2])
        rs2 = sb("rs2", [P, 2])
        x2 = [sb(f"x2_{s}", [P, 2, D]) for s in range(2)]
        x2T = sb("x2T", [P, 2, KC, T])
        logits = sb("logits", [P, B, E])
        eps = sb("eps", [P, 1])
        seen = sb("seen", [P, 2])

        w_in = [sb(f"w_in{s}", [P, W_END]) for s in range(2)]
        w_hi = sb("w_hi", [P, E, W_END], F32R)
        w_lo = sb("w_lo", [P, E, W_END], F32R)

        half = sb("half", [P, H_END], F16)
        top_l = sb("top_l", [P, B])
        shifted = sb("shifted", [P, B, E])
        expd = sb("expd", [P, B, E])
        esum = sb("esum", [P, B])
        einv = sb("einv", [P, B])
        prob = [sb(f"prob{c}", [P, B, E]) for c in range(TOPK)]
        top = sb("top", [P, TOPK, B])
        ties = sb("ties", [P, B, E])
        key = sb("key", [P, B, E])
        kmax = sb("kmax", [P, B])
        pick = sb("pick", [P, TOPK, B, E])
        chosen = sb("chosen", [P, B + 1, E], F16)
        tsum = sb("tsum", [P, B])
        tinv = sb("tinv", [P, B])
        gate = sb("gate", [P, TOPK, B])
        need = sb("need", [P, E])
        tiles_of = sb("tiles_of", [P, E])
        upto = [sb(f"upto{n}", [P, 2 * E]) for n in range(4)]
        base = sb("base", [P, E])
        place = sb("place", [P, B, E])
        placed = sb("placed", [P, TOPK, B, E])
        slot = sb("slot", [P, TOPK * B])
        part = sb("part", [P, TOPK * B])
        tile_no = sb("tile_no", [P, TOPK * B])
        row_no = sb("row_no", [P, TOPK * B])
        row_hot = sb("row_hot", [P, TOPK * B, P], F16)
        tile_hot = sb("tile_hot", [P, TOPK * B, 2, TILES], F16)
        inverse = sb("inverse", [P, 3, TILES])
        filled = sb("filled", [P, TILES])
        dest = sb("dest", [P, TILES])
        padding = sb("padding", [P, TILES])
        past = sb("past", [P, TILES, E])
        expert = sb("expert", [P, TILES])
        gather_idx = sb("gather_idx", [P, TILES], I32)
        scatter_idx = sb("scatter_idx", [P, TILES], I32)
        gather_now = [sb(f"gather_now{s}", [P, 1], I32) for s in range(RING)]
        scatter_now = [sb(f"scatter_now{s}", [P, 1], I32) for s in range(RING)]
        none = sb("none", [P, 1], I32)
        expert_idx = sb("expert_idx", [P, TILES], I32)

        xs = [sb(f"xs{s}", [P, D]) for s in range(RING)]
        xs_hi = [sb(f"xs_hi{s}", [P, KC, P], F32R) for s in range(RING)]
        xs_lo = [sb(f"xs_lo{s}", [P, KC, P], F32R) for s in range(RING)]
        silu, hid = cs[:, 0, :], cs[:, 1, :]
        hid_hi = sb("hid_hi", [P, KC, P], F32R)
        hid_lo = sb("hid_lo", [P, KC, P], F32R)
        ys = [r2[:, 0, :], r2[:, 1, :], x2T[:, 0, :, :].rearrange("p k t -> p (k t)")]

        x2_dram = nc.dram_tensor("x2_dram", (N, D), F32, kind="Internal").ap()
        y_dram = nc.dram_tensor("y_dram", (TOPK * N, D), F32, kind="Internal").ap()
        x2_pairs = x2_dram.rearrange("(j q t) d -> j t q d", q=2, t=T)
        y_pairs = y_dram.rearrange("(c j q t) d -> c j t q d", c=TOPK, q=2, t=T)

        p_v = ps("p_v", [P, 2, D])
        p_c = ps("p_c", [P, 2, 2, D])
        p_y = ps("p_y", [P, 2, D])
        p_t = ps("p_t", [P, 2, KC, T])
        p_s = ps("p_s", [P, 2 * D])
        p_a = ps("p_a", [P, 2, D])
        p_r = ps("p_r", [P, 2 * D])
        scores = p_s[:, 0:2 * T].rearrange("p (q s) -> p q s", q=2)
        rowsum = p_r[:, 0:2]
        plog = p_r[:, 64:64 + 2 * E].rearrange("p (q e) -> p q e", q=2)

        p_place = p_v[:].rearrange("p q d -> p (q d)")[:, 0:(B + 1) * E].rearrange("p (b e) -> p b e", e=E)
        p_inv = p_y[:].rearrange("p q d -> p (q d)")[:, 0:3 * TILES].rearrange("p (f k) -> p f k", f=3)
        p_up = [p_v[:], p_c[:, 0, :, :], p_c[:, 1, :, :]]
        p_xt = p_y[:].rearrange("p q d -> p (q d)")[:, 0:D].rearrange("p (k t) -> p k t", k=KC)
        p_ht = p_t[:, 0, :, :]
        p_down = [p_s[:, 0:D], p_a[:, 0, :], p_r[:, 0:D]]

        x2_in, y0_in, y1_in, res = (
            x_in, [t[:].rearrange("p q k t -> p q (k t)") for t in xT_in], [t[:] for t in c_in],
            [t[:].rearrange("p q k t -> p q (k t)") for t in cT_in])
        weighed, summed = x1, x2

        tri = const[:, C_TRI:C_TRI + P]
        ident = const[:, C_IDENT:C_IDENT + P]
        decay = const[:, C_DECAY:C_DECAY + P].rearrange("p (a s) -> p a s", a=1).to_broadcast([P, 2, T])

        const_in, proj_in, freq_in = sem("const_in"), sem("proj_in"), sem("freq_in")
        w_ok = [sem(f"w_ok{s}") for s in range(2)]
        hi_ok, lo_ok = sem("hi_ok"), sem("lo_ok")
        route, shift_ok, exp_ok, chosen_ok, place_ok = (sem(n) for n in (
            "route", "shift_ok", "exp_ok", "chosen_ok", "place_ok"))
        row_hot_ok, tile_hot_ok, inv_ok, index_ok, x2_saved = (sem(n) for n in (
            "row_hot_ok", "tile_hot_ok", "inv_ok", "index_ok", "x2_saved"))
        xs_ok = [sem(f"xs_ok{s}") for s in range(RING)]
        xt_ok, xhi_ok, xlo_ok, up_ok, silu_ok, hid_ok = (sem(n) for n in (
            "xt_ok", "xhi_ok", "xlo_ok", "up_ok", "silu_ok", "hid_ok"))
        ht_ok, hhi_ok, hlo_ok, down_ok, ys_ok = (sem(n) for n in (
            "ht_ok", "hhi_ok", "hlo_ok", "down_ok", "ys_ok"))
        gather_now_ok, scatter_now_ok, none_ok = sem("gather_now_ok"), sem("scatter_now_ok"), sem("none_ok")
        put_ok = [sem(f"put_ok{s}") for s in range(RING)]
        x2_back = [sem(f"x2_back{s}") for s in range(2)]
        y0_back = [sem(f"y0_back{s}") for s in range(2)]
        y1_back = [sem(f"y1_back{s}") for s in range(2)]
        weighed_ok, sum0_ok, r3_ok, st3_ok, mv3_ok, sd3_ok, rs3_ok, res_ok = (sem(n) for n in (
            "weighed_ok", "sum0_ok", "r3_ok", "st3_ok", "mv3_ok", "sd3_ok", "rs3_ok", "res_ok"))
        out_ok = [sem(f"out_ok{s}") for s in range(2)]
        x_ok = [sem(f"x_ok{s}") for s in range(2)]
        xT_ok = [sem(f"xT_ok{s}") for s in range(2)]
        c_ok = [sem(f"c_ok{s}") for s in range(2)]
        cT_ok = [sem(f"cT_ok{s}") for s in range(2)]
        angle_ok, rotor_ok = sem("angle_ok"), sem("rotor_ok")
        eps_ok = sem("eps_ok")
        v_ok, turned_ok, sums_ok, back_ok, got_ok, y_ok = (sem(n) for n in (
            "v_ok", "turned_ok", "sums_ok", "back_ok", "got_ok", "y_ok"))
        r1_ok, st1_ok, mv1_ok, sd1_ok, rs1_ok, x1_ok = (sem(n) for n in (
            "r1_ok", "st1_ok", "mv1_ok", "sd1_ok", "rs1_ok", "x1_ok"))
        t1_ok, x1T_ok, sc_ok, att_ok, sum_ok, vabs_ok, vmax_ok, vinv_ok, cs_ok, av_ok = (sem(n) for n in (
            "t1_ok", "x1T_ok", "sc_ok", "att_ok", "sum_ok", "vabs_ok", "vmax_ok", "vinv_ok", "cs_ok", "av_ok"))
        r2_ok, st2_ok, mv2_ok, sd2_ok, rs2_ok, x2_ok = (sem(n) for n in (
            "r2_ok", "st2_ok", "mv2_ok", "sd2_ok", "rs2_ok", "x2_ok"))
        t2_ok, x2T_ok, lg_ok, logits_ok = (sem(n) for n in ("t2_ok", "x2T_ok", "lg_ok", "logits_ok"))
        x2_free = sem("x2_free")
        x2_out = [sem(f"x2_out{s}") for s in range(2)]

        def pipeline(engine, step):
            def fixed(i):
                step(i, i % 2, lambda k: 0 <= i + k < PAIRS)
            for i in range(-1, 2):
                fixed(i)
            with engine.Fori(1, PAIRS // 2 - 1) as half:
                step(2 * half, 0, lambda k: True)
                step(2 * half + 1, 1, lambda k: True)
            for i in range(PAIRS - 2, PAIRS + 2):
                fixed(i)

        def tile_pipeline(engine, step):
            def fixed(k):
                step(k, lambda d: ((k + d) % RING, (k + d) // RING), lambda d: 0 <= k + d < TILES)
            for k in range(-1, 2 * RING):
                fixed(k)
            with engine.Fori(2, TILES // RING - 2) as trip:
                for u in range(RING):
                    step(RING * trip + u, lambda d: ((u + d) % RING, trip + (u + d) // RING), lambda d: True)
            for k in range(RING * (TILES // RING - 2), TILES + 3):
                fixed(k)

        block = scope.enter_context(nc.Block())

        @block.sync
        def _(sp):
            sp.dma_start(frow[:], freq_row).then_inc(freq_in, 16)
            sp.dma_start(fcol[:], freq_col).then_inc(freq_in, 16)
            sp.dma_start(const[:], consts).then_inc(const_in, 16)
            sp.dma_start(half[:], halves).then_inc(const_in, 16)
            sp.dma_start(wv[:], wvT).then_inc(proj_in, 16)

            def step(i, s, has):
                j = i + 2
                if has(2):
                    for tile, src, ok, free in ((xT_in, xT, xT_ok, v_ok), (x_in, x, x_ok, r1_ok),
                                                (cT_in, ctxT, cT_ok, sc_ok), (c_in, ctxt, c_ok, cs_ok),
                                                (w_in, weights, w_ok, lo_ok)):
                        if has(0):
                            sp.wait_ge(free, i + 1)
                        sp.dma_start(tile[s][:], src[bass.ds(j, 1), :, :].rearrange("a p n -> p (a n)")).then_inc(ok[s], 16)
                if has(-2):
                    sp.wait_ge(x2_ok, i - 1)
                    sp.dma_start(x2_pairs[bass.ds(i - 2, 1), :, :, :].rearrange("a t q d -> t (a q) d"),
                                 x2[s][:]).then_inc(x2_out[s], 16)
                    sp.wait_ge(x2_out[s], 8 * (i - s))
                    sp.sem_inc(x2_free, 1)

            sp.sem_inc(x2_free, 2)
            step(-2, 0, lambda k: k == 2)
            sp.dma_start(wo[:], woT).then_inc(proj_in, 16)
            sp.dma_start(wr[:], routerT).then_inc(proj_in, 16)
            pipeline(sp, step)
            sp.sem_inc(x2_saved, 1)

            for s in range(RING):
                sp.wait_ge(put_ok[s], 16 * (TILES // RING))

            def finish(i, s, has):
                if has(2):
                    if has(0):
                        sp.wait_ge(r3_ok, i + 1)
                    sp.dma_start(x2_in[s][:],
                                 x2_pairs[bass.ds(i + 2, 1), :, :, :].rearrange("a t q d -> t (a q) d")).then_inc(x2_back[s], 16)
                    sp.dma_start(y0_in[s], y_pairs[0, bass.ds(i + 2, 1), :, :, :].rearrange("a t q d -> t (a q) d")).then_inc(y0_back[s], 16)
                    sp.dma_start(y1_in[s], y_pairs[1, bass.ds(i + 2, 1), :, :, :].rearrange("a t q d -> t (a q) d")).then_inc(y1_back[s], 16)
                if has(0):
                    sp.wait_ge(res_ok, i + 1)
                    sp.dma_start(out[bass.ds(i, 1), :, :].rearrange("a p n -> p (a n)"), res[s].rearrange("p q d -> p (q d)")).then_inc(out_ok[s], 16)

            finish(-2, 0, lambda k: k == 2)
            pipeline(sp, finish)
            for s in range(2):
                sp.wait_ge(out_ok[s], 16 * PAIRS // 2)

        @block.tensor
        def _(pe):
            pe.wait_ge(const_in, 32)
            pe.wait_ge(proj_in, 48)

            def values(j, s, nth, first):
                pe.wait_ge(xT_ok[s], nth)
                if not first:
                    pe.wait_ge(turned_ok, j)
                for q in range(2):
                    for k in range(KC):
                        last = nc.tensor.matmul(p_v[:, q, :], xT_in[s][:, q, k, :], wv[:, k, :],
                                                start=(k == 0), stop=(k == KC - 1))
                last.then_inc(v_ok, 1)

            def step(i, s, has):
                if has(0):
                    pe.wait_ge(turned_ok, i + 1)
                    for q in range(2):
                        for h in range(2):
                            for k in range(KC):
                                last = nc.tensor.matmul(p_c[:, q, h, k * T:(k + 1) * T],
                                                        turned[:, q, h, k * P:(k + 1) * P], tri,
                                                        start=True, stop=True)
                    last.then_inc(sums_ok, 1)
                if has(-1):
                    pe.wait_ge(x1_ok, i)
                    for q in range(2):
                        for k in range(KC):
                            last = nc.tensor.transpose(p_t[:, q, k, :], x1[1 - s][:, q, k * P:(k + 1) * P], ident)
                    last.then_inc(t1_ok, 1)
                if has(1):
                    values(i + 1, 1 - s, 8 * (i + s) + 16,
                           isinstance(i, int) and i == -1)
                if has(-1):
                    pe.wait_ge(cT_ok[1 - s], 8 * (i - 1 - (1 - s)) + 16)
                    pe.wait_ge(x1T_ok, i)
                    if has(-2):
                        pe.wait_ge(att_ok, i - 1)
                    for q in range(2):
                        for k in range(KC):
                            last = nc.tensor.matmul(scores[:, q, :], cT_in[1 - s][:, q, k, :], x1T[:, q, k, :],
                                                    start=(k == 0), stop=(k == KC - 1))
                    last.then_inc(sc_ok, 1)
                if has(-2):
                    pe.wait_ge(x2_ok, i - 1)
                    if has(-1):
                        pe.wait_ge(x1T_ok, i)
                    for q in range(2):
                        for k in range(KC):
                            last = nc.tensor.transpose(p_t[:, q, k, :], x2[s][:, q, k * P:(k + 1) * P], ident)
                    last.then_inc(t2_ok, 1)
                if has(-1):
                    pe.wait_ge(att_ok, i)
                    if has(-3):
                        pe.wait_ge(logits_ok, i - 2)
                    for q in range(2):
                        last = nc.tensor.matmul(rowsum[:, q:q + 1], att[:, q, :], const[:, C_ONE:C_ONE + 1],
                                                start=True, stop=True)
                    last.then_inc(sum_ok, 1)
                if has(0):
                    pe.wait_ge(got_ok, i + 1)
                    for q in range(2):
                        for k in range(KC):
                            last = nc.tensor.matmul(p_y[:, q, :], got[:, q, k, :], wo[:, k, :],
                                                    start=(k == 0), stop=(k == KC - 1))
                    last.then_inc(y_ok, 1)
                if has(-2):
                    pe.wait_ge(x2T_ok, i - 1)
                    if has(-1):
                        pe.wait_ge(vabs_ok, i)
                    for q in range(2):
                        for k in range(KC):
                            last = nc.tensor.matmul(plog[:, q, :], x2T[:, q, k, :], wr[:, k, :],
                                                    start=(k == 0), stop=(k == KC - 1))
                    last.then_inc(lg_ok, 1)
                if has(-1):
                    pe.wait_ge(cs_ok, i)
                    if has(-2):
                        pe.wait_ge(r2_ok, i - 1)
                    for q in range(2):
                        last = nc.tensor.matmul(p_a[:, q, :], att[:, q, :], cs[:, q, :], start=True, stop=True)
                    last.then_inc(av_ok, 1)

            pipeline(pe, step)

            pe.wait_ge(chosen_ok, 2)
            nc.tensor.matmul(p_place, half[:, H_STRICT:H_STRICT + P], chosen[:], start=True, stop=True, skip_group_check=True)
            for b in range(B):
                last = nc.tensor.matmul(p_place[:, b + 1:, :], half[:, H_ONES:H_ONES + P],
                                        chosen[:, b:b + 1, :].to_broadcast([P, B - b, E]),
                                        start=False, stop=True, skip_group_check=True)
            last.then_inc(place_ok, 1)
            pe.wait_ge(tile_hot_ok, 2)
            for n in range(TOPK * B):
                pe.wait_ge(row_hot_ok, n + 1)
                flags = p_inv[:, 0:2, :] if n < B else p_inv[:, 0:3:2, :]
                last = nc.tensor.matmul(flags, row_hot[:, n, :], tile_hot[:, n, :, :],
                                        start=(n == 0), stop=True, skip_group_check=True)
            last.then_inc(inv_ok, 1)
            pe.wait_ge(index_ok, 3)

            def split_product(dst, lhs_hi, lhs_lo, col, width, which):
                n = 0
                for lhs, w in ((lhs_hi, w_hi), (lhs_hi, w_lo), (lhs_lo, w_hi)):
                    for k in range(KC):
                        at = col + k * width
                        last = nc.tensor.matmul(dst, lhs[:, k, :],
                                                w[:, bass.ds(which, 1), at:at + width].rearrange("p a n -> p (a n)"),
                                                start=(n == 0), stop=(n == 3 * KC - 1))
                        n += 1
                return last

            def tile(k, at, has):
                if has(1):
                    s, used = at(1)
                    pe.wait_ge(xs_ok[s], 16 * used + 16)
                    if has(0):
                        pe.wait_ge(xlo_ok, k + 1)
                    for c in range(KC):
                        last = nc.tensor.transpose(p_xt[:, c, :], xs[s][:, c * P:(c + 1) * P], ident)
                    last.then_inc(xt_ok, 1)
                if has(-2):
                    s, _ = at(-2)
                    which = pe.value_load(expert_idx[0:1, bass.ds(k - 2, 1)], min_val=0, max_val=E - 1)
                    pe.wait_ge(hlo_ok, k - 1)
                    if has(-5):
                        pe.wait_ge(ys_ok, k - 4)
                    split_product(p_down[s], hid_hi, hid_lo, W_DOWN, D, which).then_inc(down_ok, 1)
                if has(-1):
                    pe.wait_ge(hid_ok, k)
                    for c in range(KC):
                        last = nc.tensor.transpose(p_ht[:, c, :], hid[:, c * P:(c + 1) * P], ident)
                    last.then_inc(ht_ok, 1)
                if has(0):
                    s, _ = at(0)
                    which = pe.value_load(expert_idx[0:1, bass.ds(k, 1)], min_val=0, max_val=E - 1)
                    pe.wait_ge(xlo_ok, k + 1)
                    if has(-3):
                        pe.wait_ge(hid_ok, k - 2)
                    split_product(p_up[s], xs_hi[s], xs_lo[s], W_UP, 2 * DH, which).then_inc(up_ok, 1)

            tile_pipeline(pe, tile)

        @block.vector
        def _(dve):
            dve.wait_ge(const_in, 32)
            dve.wait_ge(freq_in, 32)
            nc.vector.memset(eps[:], EPS).then_inc(eps_ok, 1)
            tok = const[:, C_TOK:C_TOK + 1]
            nc.vector.tensor_scalar(angle[:, 0, :], frow[:], tok, None, ALU.mult).then_inc(angle_ok, 1)
            for k in range(KC):
                nc.vector.tensor_scalar(angle[:, 1, k * T:(k + 1) * T], const[:, C_ROW:C_ROW + P],
                                        fcol[:, k:k + 1], None, ALU.mult).then_inc(angle_ok, 1)
            done = 1 + KC
            dve.wait_ge(angle_ok, done)
            nc.vector.tensor_scalar(turns[:], angle[:], 1.0 / TWO_PI, ROUND, ALU.mult, ALU.add).then_inc(angle_ok, 1)
            dve.wait_ge(angle_ok, done + 1)
            nc.vector.tensor_scalar(rem[:], turns[:], -ROUND, None, ALU.add).then_inc(angle_ok, 1)
            dve.wait_ge(angle_ok, done + 2)
            nc.vector.scalar_tensor_tensor(turns[:], rem[:], -TURN_HI, angle[:], ALU.mult, ALU.add).then_inc(angle_ok, 1)
            dve.wait_ge(angle_ok, done + 3)
            nc.vector.scalar_tensor_tensor(angle[:], rem[:], -TURN_MID, turns[:], ALU.mult, ALU.add).then_inc(angle_ok, 1)
            dve.wait_ge(angle_ok, done + 4)
            nc.vector.scalar_tensor_tensor(turns[:], rem[:], -TURN_LO, angle[:], ALU.mult, ALU.add).then_inc(angle_ok, 1)
            dve.wait_ge(angle_ok, done + 5)
            nc.vector.tensor_scalar(angle[:], turns[:], SIN_MAX, -SIN_MAX, ALU.min, ALU.max).then_inc(angle_ok, 1)
            dve.wait_ge(angle_ok, done + 6)
            nc.vector.scalar_tensor_tensor(turns[:], angle[:], -1.0, angle[:], ALU.mult, ALU.min).then_inc(angle_ok, 1)
            dve.wait_ge(angle_ok, done + 7)
            nc.vector.tensor_scalar(rem[:], turns[:], np.pi / 2, None, ALU.add).then_inc(angle_ok, 1)

            def norm(i, src, st, mv, sd, rs, dst, r_ok, st_ok, mv_ok, sd_ok, rs_ok, dst_ok):
                dve.wait_ge(r_ok, i + 1)
                for q in range(2):
                    nc.vector.bn_stats(st[:, q, :], src[:, q, :]).then_inc(st_ok, 1)
                dve.wait_ge(st_ok, 2 * i + 2)
                nc.vector.tensor_copy(seen[:], st[:, :, 0]).then_inc(mv_ok, 1)
                for q in range(2):
                    nc.vector.bn_aggr(mv[:, q, :], st[:, q, :]).then_inc(mv_ok, 1)
                dve.wait_ge(sd_ok, i + 1)
                nc.vector.reciprocal(rs[:], sd[:]).then_inc(rs_ok, 1)
                dve.wait_ge(rs_ok, i + 1)
                for q in range(2):
                    last = nc.vector.tensor_scalar(dst[:, q, :], src[:, q, :], mv[:, q, 0:1], rs[:, q:q + 1],
                                                   ALU.subtract, ALU.mult)
                last.then_inc(dst_ok, 1)

            def turn(j):
                dve.wait_ge(v_ok, j + 1)
                for q in range(2):
                    last = nc.vector.tensor_tensor(
                        turned[:, q, :, :], p_v[:, q:q + 1, :].to_broadcast([P, 2, D]), rotor[:, 0, :, :], ALU.mult)
                last.then_inc(turned_ok, 1)

            def step(i, s, has):
                if has(0):
                    dve.wait_ge(sums_ok, i + 1)
                    if has(-1):
                        dve.wait_ge(got_ok, i)
                    for q in range(2):
                        last = nc.vector.tensor_tensor(back[:, q, :, :], p_c[:, q, :, :], rotor[:, 1, :, :], ALU.mult)
                    last.then_inc(back_ok, 1)
                if has(-2):
                    dve.wait_ge(av_ok, i - 1)
                    nc.vector.tensor_tensor(r2[:], p_a[:], x1[s][:], ALU.add).then_inc(r2_ok, 1)
                    dve.wait_ge(x2_free, i - 1)
                    norm(i - 2, r2, st2, mv2, sd2, rs2, x2[s], r2_ok, st2_ok, mv2_ok, sd2_ok, rs2_ok, x2_ok)
                if has(1):
                    if isinstance(i, int) and i == -1:
                        dve.wait_ge(rotor_ok, 2)
                    turn(i + 1)
                if has(-1):
                    dve.wait_ge(sc_ok, i)
                    nc.vector.tensor_tensor(att[:], scores, decay, ALU.mult).then_inc(att_ok, 1)
                    dve.wait_ge(vabs_ok, i)
                    nc.vector.tensor_scalar(vmax[:], vabs[:], 1.0, None, ALU.max).then_inc(vmax_ok, 1)
                    dve.wait_ge(vmax_ok, i)
                    nc.vector.reciprocal(vinv[:], vmax[:]).then_inc(vinv_ok, 1)
                if has(0):
                    dve.wait_ge(y_ok, i + 1)
                    dve.wait_ge(x_ok[s], 8 * (i - s) + 16)
                    nc.vector.tensor_tensor(r1[:], p_y[:], x_in[s][:], ALU.add).then_inc(r1_ok, 1)
                    norm(i, r1, st1, mv1, sd1, rs1, x1[s], r1_ok, st1_ok, mv1_ok, sd1_ok, rs1_ok, x1_ok)

            pipeline(dve, step)

            count = [0]

            def link(ins):
                count[0] += 1
                ins.then_inc(route, 1)
                dve.wait_ge(route, count[0])

            def over_e(v):
                return v.unsqueeze(2).to_broadcast([P, B, E])

            nc.vector.memset(chosen[:, B, :], 0.0).then_inc(chosen_ok, 1)
            for n in range(4):
                link(nc.vector.memset(upto[n][:], 0.0))
            dve.wait_ge(logits_ok, PAIRS)
            link(nc.vector.tensor_reduce(top_l[:], logits[:], AX_X, ALU.max))
            nc.vector.tensor_tensor(shifted[:], logits[:], over_e(top_l[:]), ALU.subtract).then_inc(shift_ok, 1)
            dve.wait_ge(exp_ok, 1)
            link(nc.vector.tensor_reduce(esum[:], expd[:], AX_X, ALU.add))
            link(nc.vector.reciprocal(einv[:], esum[:]))
            link(nc.vector.tensor_tensor(prob[0][:], expd[:], over_e(einv[:]), ALU.mult))
            for c in range(TOPK):
                link(nc.vector.tensor_reduce(top[:, c, :], prob[c][:], AX_X, ALU.max))
                link(nc.vector.tensor_tensor(ties[:], prob[c][:], over_e(top[:, c, :]), ALU.is_equal))
                pref = const[:, C_PREF:C_PREF + E].unsqueeze(1).to_broadcast([P, B, E])
                link(nc.vector.tensor_tensor(key[:], ties[:], pref, ALU.mult))
                link(nc.vector.tensor_reduce(kmax[:], key[:], AX_X, ALU.max))
                link(nc.vector.tensor_tensor(pick[:, c, :, :], key[:], over_e(kmax[:]), ALU.is_equal))
                if c == 0:
                    link(nc.vector.scalar_tensor_tensor(prob[1][:], pick[:, 0, :, :], -4.0, prob[0][:], ALU.mult, ALU.add))
            nc.vector.tensor_tensor(chosen[:, 0:B, :], pick[:, 0, :, :], pick[:, 1, :, :], ALU.add).then_inc(chosen_ok, 1)
            link(nc.vector.tensor_tensor(tsum[:], top[:, 0, :], top[:, 1, :], ALU.add))
            link(nc.vector.reciprocal(tinv[:], tsum[:]))
            link(nc.vector.tensor_tensor(gate[:], top[:], tinv[:].unsqueeze(1).to_broadcast([P, TOPK, B]), ALU.mult))
            dve.wait_ge(place_ok, 1)
            link(nc.vector.tensor_scalar(need[:], p_place[:, B, :], HALF, 1.0 / P, ALU.add, ALU.mult))
            link(nc.vector.tensor_scalar(tiles_of[:], need[:], ROUND, -ROUND, ALU.add, ALU.add))
            link(nc.vector.tensor_copy(upto[0][:, E:], tiles_of[:]))
            for n in range(3):
                back_by = 2 ** n
                link(nc.vector.tensor_tensor(upto[n + 1][:, E:], upto[n][:, E:], upto[n][:, E - back_by:2 * E - back_by], ALU.add))
            link(nc.vector.tensor_tensor(base[:], upto[3][:, E:], tiles_of[:], ALU.subtract))
            link(nc.vector.tensor_scalar(need[:], base[:], float(P), None, ALU.mult))
            link(nc.vector.tensor_tensor(place[:], p_place[:, 0:B, :], need[:].unsqueeze(1).to_broadcast([P, B, E]), ALU.add))
            link(nc.vector.tensor_tensor(placed[:], pick[:], place[:].unsqueeze(1).to_broadcast([P, TOPK, B, E]), ALU.mult))
            link(nc.vector.tensor_reduce(slot[:], placed[:].rearrange("p c b e -> p (c b) e"), AX_X, ALU.add))
            link(nc.vector.tensor_scalar(part[:], slot[:], -HALF, 1.0 / P, ALU.add, ALU.mult))
            link(nc.vector.tensor_scalar(tile_no[:], part[:], ROUND, -ROUND, ALU.add, ALU.add))
            link(nc.vector.scalar_tensor_tensor(row_no[:], tile_no[:], -float(P), slot[:], ALU.mult, ALU.add))
            tiles_row = const[:, C_ROW:C_ROW + TILES].unsqueeze(1).to_broadcast([P, TOPK * B, TILES])
            nc.vector.tensor_tensor(tile_hot[:, :, 1, :], tiles_row,
                                    tile_no[:].unsqueeze(2).to_broadcast([P, TOPK * B, TILES]),
                                    ALU.is_equal).then_inc(tile_hot_ok, 1)
            dve.wait_ge(tile_hot_ok, 1)
            for c in range(TOPK):
                tokens = const[:, C_TOKID:C_TOKID + B].unsqueeze(2).to_broadcast([P, B, TILES])
                last = nc.vector.tensor_tensor(tile_hot[:, c * B:(c + 1) * B, 0, :], tile_hot[:, c * B:(c + 1) * B, 1, :],
                                               tokens, ALU.mult)
            last.then_inc(tile_hot_ok, 1)
            for n in range(TOPK * B):
                nc.vector.tensor_scalar(row_hot[:, n, :], half[:, H_ROW:H_ROW + P], row_no[:, n:n + 1], None,
                                        ALU.is_equal).then_inc(row_hot_ok, 1)
            link(nc.vector.tensor_tensor(past[:], const[:, C_ROW:C_ROW + TILES].unsqueeze(2).to_broadcast([P, TILES, E]),
                                         upto[3][:, E:].unsqueeze(1).to_broadcast([P, TILES, E]), ALU.is_ge))
            link(nc.vector.tensor_reduce(expert[:], past[:], AX_X, ALU.add))
            nc.vector.tensor_scalar(expert_idx[:], expert[:], float(E - 1), None, ALU.min).then_inc(index_ok, 1)
            dve.wait_ge(inv_ok, 1)
            nc.vector.tensor_copy(gather_idx[:], p_inv[:, 0, :]).then_inc(index_ok, 1)
            link(nc.vector.tensor_copy(inverse[:], p_inv))
            link(nc.vector.tensor_tensor(filled[:], inverse[:, 1, :], inverse[:, 2, :], ALU.add))
            link(nc.vector.scalar_tensor_tensor(dest[:], inverse[:, 2, :], float(N), inverse[:, 0, :], ALU.mult, ALU.add))
            link(nc.vector.tensor_scalar(padding[:], filled[:], -float(SKIP), float(SKIP), ALU.mult, ALU.add))
            nc.vector.tensor_tensor(scatter_idx[:], dest[:], padding[:], ALU.add).then_inc(index_ok, 1)

            def tile(k, at, has):
                if has(1):
                    s, _ = at(1)
                    dve.wait_ge(xhi_ok, k + 2)
                    nc.vector.tensor_tensor(xs_lo[s][:], p_xt, xs_hi[s][:].bitcast(F32), ALU.subtract).then_inc(xlo_ok, 1)
                if has(-1):
                    dve.wait_ge(hhi_ok, k)
                    nc.vector.tensor_tensor(hid_lo[:], p_ht, hid_hi[:].bitcast(F32), ALU.subtract).then_inc(hlo_ok, 1)
                if has(0):
                    s, _ = at(0)
                    dve.wait_ge(silu_ok, k + 1)
                    up_rows = p_up[s].rearrange("p q d -> p (q d)")[:, DH:2 * DH]
                    nc.vector.tensor_tensor(hid, up_rows, silu, ALU.mult).then_inc(hid_ok, 1)

            tile_pipeline(dve, tile)

            def finish(i, s, has):
                if has(0):
                    dve.wait_ge(sum0_ok, i + 1)
                    dve.wait_ge(y1_back[s], 8 * (i - s) + 16)
                    if has(-1):
                        dve.wait_ge(res_ok, i)
                    for q in range(2):
                        last = nc.vector.scalar_tensor_tensor(
                            r1[:, q, :], y1_in[s][:, q, :], gate[:, 1, bass.ds(2 * i + q, 1)], summed[s][:, q, :],
                            ALU.mult, ALU.add)
                    last.then_inc(r3_ok, 1)
                    if has(-2):
                        dve.wait_ge(out_ok[s], 8 * (i - s))
                    norm(i, r1, st1, mv1, sd1, rs1, res[s], r3_ok, st3_ok, mv3_ok, sd3_ok, rs3_ok, res_ok)

            pipeline(dve, finish)

        @block.scalar
        def _(act):
            act.wait_ge(angle_ok, 1 + KC + 7)
            nc.scalar.activation(rotor[:, :, 1, :], angle[:], ACT.Sin).then_inc(rotor_ok, 1)
            act.wait_ge(angle_ok, 1 + KC + 8)
            nc.scalar.activation(rotor[:, :, 0, :], rem[:], ACT.Sin).then_inc(rotor_ok, 1)
            act.wait_ge(eps_ok, 1)

            def step(i, s, has):
                if has(-2):
                    act.wait_ge(mv2_ok, 3 * i - 3)
                    nc.scalar.activation(sd2[:], mv2[:, :, 1], ACT.Sqrt, bias=eps[:]).then_inc(sd2_ok, 1)
                if has(-1):
                    act.wait_ge(t1_ok, i)
                    nc.scalar.activation(x1T[:], p_t[:], ACT.Copy).then_inc(x1T_ok, 1)
                if has(-2):
                    act.wait_ge(t2_ok, i - 1)
                    nc.scalar.activation(x2T[:], p_t[:], ACT.Copy).then_inc(x2T_ok, 1)
                if has(-1):
                    act.wait_ge(sum_ok, i)
                    nc.scalar.activation(vabs[:], rowsum, ACT.Abs).then_inc(vabs_ok, 1)
                if has(-2):
                    act.wait_ge(lg_ok, i - 1)
                    nc.scalar.activation(logits[:, bass.ds(2 * (i - 2), 2), :], plog, ACT.Copy).then_inc(logits_ok, 1)
                if has(0):
                    act.wait_ge(mv1_ok, 3 * i + 3)
                    nc.scalar.activation(sd1[:], mv1[:, :, 1], ACT.Sqrt, bias=eps[:]).then_inc(sd1_ok, 1)

                if has(0):
                    act.wait_ge(w_ok[s], 8 * (i - s) + 16)
                    nc.scalar.activation(w_hi[:, bass.ds(i, 1), :].rearrange("p a n -> p (a n)"), w_in[s][:],
                                         ACT.Copy).then_inc(hi_ok, 1)

            pipeline(act, step)

            act.wait_ge(shift_ok, 1)
            nc.scalar.activation(expd[:], shifted[:], ACT.Exp).then_inc(exp_ok, 1)

            def tile(k, at, has):
                if has(1):
                    s, _ = at(1)
                    act.wait_ge(xt_ok, k + 2)
                    nc.scalar.activation(xs_hi[s][:], p_xt, ACT.Copy).then_inc(xhi_ok, 1)
                if has(-2):
                    s, used = at(-2)
                    act.wait_ge(down_ok, k - 1)
                    if has(-5):
                        act.wait_ge(put_ok[s], 16 * used)
                    nc.scalar.activation(ys[s], p_down[s], ACT.Copy).then_inc(ys_ok, 1)
                if has(-1):
                    act.wait_ge(ht_ok, k)
                    nc.scalar.activation(hid_hi[:], p_ht, ACT.Copy).then_inc(hhi_ok, 1)
                if has(0):
                    s, _ = at(0)
                    act.wait_ge(up_ok, k + 1)
                    gate_rows = p_up[s].rearrange("p q d -> p (q d)")[:, 0:DH]
                    nc.scalar.activation(silu, gate_rows, ACT.Silu).then_inc(silu_ok, 1)

            tile_pipeline(act, tile)

            def finish(i, s, has):
                if has(0):
                    act.wait_ge(y0_back[s], 8 * (i - s) + 16)
                    for q in range(2):
                        nc.scalar.activation(weighed[s][:, q, :], y0_in[s][:, q, :], ACT.Copy,
                                             scale=gate[:, 0, bass.ds(2 * i + q, 1)]).then_inc(weighed_ok, 1)
                    act.wait_ge(mv3_ok, 3 * i + 3)
                    nc.scalar.activation(sd1[:], mv1[:, :, 1], ACT.Sqrt, bias=eps[:]).then_inc(sd3_ok, 1)

            pipeline(act, finish)

        @block.gpsimd
        def _(pool):
            def step(i, s, has):
                if has(0):
                    pool.wait_ge(back_ok, i + 1)
                    if has(-1):
                        pool.wait_ge(y_ok, i)
                    nc.gpsimd.tensor_tensor(got[:], back[:, :, 0, :].rearrange("p q (k t) -> p q k t", k=KC),
                                            back[:, :, 1, :].rearrange("p q (k t) -> p q k t", k=KC), ALU.add).then_inc(got_ok, 1)
                if has(-1):
                    pool.wait_ge(c_ok[1 - s], 8 * (i - 1 - (1 - s)) + 16)
                    pool.wait_ge(vinv_ok, i)
                    if has(-2):
                        pool.wait_ge(av_ok, i - 1)
                    for q in range(2):
                        last = nc.gpsimd.tensor_tensor(cs[:, q, :], c_in[1 - s][:, q, :], vinv[:, q:q + 1].to_broadcast([P, D]), ALU.mult)
                    last.then_inc(cs_ok, 1)

                if has(0):
                    pool.wait_ge(hi_ok, i + 1)
                    nc.gpsimd.tensor_tensor(w_lo[:, bass.ds(i, 1), :].rearrange("p a n -> p (a n)"), w_in[s][:],
                                            w_hi[:, bass.ds(i, 1), :].rearrange("p a n -> p (a n)").bitcast(F32),
                                            ALU.subtract).then_inc(lo_ok, 1)

            pipeline(pool, step)

            def gather_from(k, s):
                nc.gpsimd.tensor_tensor(gather_now[s][:], gather_idx[:, bass.ds(k, 1)], none[:], ALU.add).then_inc(gather_now_ok, 1)

            def gather(s):
                nc.gpsimd.indirect_dma_start(xs[s][:], None, x2_dram,
                                             bass.IndirectOffsetOnAxis(ap=gather_now[s][:], axis=0)).then_inc(xs_ok[s], 16)

            nc.gpsimd.memset(none[:], 0).then_inc(none_ok, 1)
            pool.wait_ge(none_ok, 1)
            pool.wait_ge(index_ok, 3)
            for k in range(RING):
                gather_from(k, k)
            pool.wait_ge(gather_now_ok, RING)
            pool.wait_ge(x2_saved, 1)
            for k in range(RING):
                gather(k)

            def tile(k, at, has):
                if has(4):
                    pool.wait_ge(xt_ok, k + 2)
                    if has(-3):
                        pool.wait_ge(scatter_now_ok, k - 2)
                    gather_from(k + 4, at(1)[0])
                if has(-3):
                    s, _ = at(-3)
                    if not has(4):
                        pool.wait_ge(scatter_now_ok, k - 2)
                    nc.gpsimd.indirect_dma_start(
                        y_dram, bass.IndirectOffsetOnAxis(ap=scatter_now[s][:], axis=0),
                        ys[s], None, bounds_check=TOPK * N - 1, oob_is_err=False).then_inc(put_ok[s], 16)
                if has(-2):
                    s, _ = at(-2)
                    if has(4):
                        pool.wait_ge(gather_now_ok, k + 5)
                    pool.wait_ge(ys_ok, k - 1)
                    nc.gpsimd.tensor_tensor(scatter_now[s][:], scatter_idx[:, bass.ds(k - 2, 1)], none[:], ALU.add).then_inc(scatter_now_ok, 1)
                if has(4):
                    if not has(-2):
                        pool.wait_ge(gather_now_ok, k + 5)
                    gather(at(1)[0])

            tile_pipeline(pool, tile)

            def finish(i, s, has):
                if has(0):
                    pool.wait_ge(weighed_ok, 2 * i + 2)
                    pool.wait_ge(x2_back[s], 8 * (i - s) + 16)
                    nc.gpsimd.tensor_tensor(summed[s][:], weighed[s][:], x2_in[s][:], ALU.add).then_inc(sum0_ok, 1)

            pipeline(pool, finish)


def kernel(**inputs):
    import numpy as _np
    import concourse.bacc as _bacc
    from concourse import mybir as _mybir
    from concourse.bass_utils import run_bass_kernel_spmd as _run

    a = {k: _np.asarray(v) for k, v in inputs.items()}

    def rows(v):
        return v.reshape(PAIRS, 2, T, D).transpose(0, 2, 1, 3).reshape(PAIRS, P, 2 * D)

    def columns(v):
        return v.reshape(PAIRS, 2, T, KC, P).transpose(0, 4, 1, 3, 2).reshape(PAIRS, P, 2 * D)

    def chunked(v):
        return v.reshape(KC, P, v.shape[-1]).transpose(1, 0, 2)

    consts, halves = shape_constants()
    freqs = a["L0_attn_freqs"]
    arrays = {
        "x": rows(a["x"]), "xT": columns(a["x"]),
        "ctxt": rows(a["ctx_1024"]), "ctxT": columns(a["ctx_1024"]),
        "wvT": chunked(a["L0_attn_Wv"].T), "woT": chunked(a["L0_attn_Wo"].T),
        "freq_row": _np.broadcast_to(freqs, (P, D)), "freq_col": freqs.reshape(KC, P).T,
        "routerT": chunked(a["L0_ffn_router_w"].T),
        "weights": _np.concatenate([
            a["L0_ffn_up_proj"].reshape(E, KC, P, 2 * DH).transpose(0, 2, 1, 3).reshape(E, P, W_DOWN),
            a["L0_ffn_down_proj"].reshape(E, KC, P, D).transpose(0, 2, 1, 3).reshape(E, P, KC * D)], axis=2),
        "consts": consts, "halves": halves,
    }
    arrays = {k: _np.ascontiguousarray(v) for k, v in arrays.items()}
    nc = _bacc.Bacc("TRN2", target_bir_lowering=False, num_devices=1)
    args = {k: nc.dram_tensor(f"in_{k}", v.shape, _mybir.dt.from_np(v.dtype), kind="ExternalInput").ap()
            for k, v in arrays.items()}
    out = nc.dram_tensor("out_0", (PAIRS, P, 2 * D), _mybir.dt.float32, kind="ExternalOutput").ap()
    decoder_block(nc, out=out, **args)
    r = _run(nc, [{f"in_{k}": v for k, v in arrays.items()}], core_ids=[0])
    got = r.results[0]["out_0"]
    return got.reshape(PAIRS, P, 2, D).transpose(0, 2, 1, 3).reshape(B, T, D)
```

```python
from contextlib import ExitStack

import numpy as np

import concourse.bass as bass
from concourse import mybir

ALU = mybir.AluOpType
ACT = mybir.ActivationFunctionType
AX_X = mybir.AxisListType.X
F32 = mybir.dt.float32
F32R = mybir.dt.float32r
F16 = mybir.dt.float16
I32 = mybir.dt.int32

P = 128
B, T, D = 16, 128, 256
KC = D // P
PAIRS = B // 2
E, DH = 8, 256
TOPK = 2
N = B * T
TILES = (N * TOPK + E * (P - 1)) // P
EPS = 1e-5
GAMMA = 0.96875
MASKED = 1e30
SKIP = 4 * N

ROUND = 12582912.0
TWO_PI = 2.0 * np.pi
TURN_HI = 6.28125
TURN_MID = float(np.float32(np.round((TWO_PI - TURN_HI) * 2.0 ** 21) / 2.0 ** 21))
TURN_LO = float(np.float32(TWO_PI - TURN_HI - TURN_MID))
SIN_MAX = 3.1415925

C_DECAY, C_TRI, C_IDENT, C_ONE, C_TOK, C_ROW = 0, P, 2 * P, 3 * P, 3 * P + 1, 3 * P + 2
C_CODE = C_ROW + P
C_PREF = C_CODE + TOPK * B
C_END = C_PREF + E
H_STRICT, H_ONES, H_ROW, H_END = 0, P, 2 * P, 3 * P
W_UP, W_DOWN = 0, KC * 2 * DH
W_END = W_DOWN + KC * D
AHEAD = 3
RING = 3
UNROLL = 3 * RING
HALF = 63.5


def shape_constants():
    i = np.arange(P)
    decay = np.where(i[:, None] >= i[None, :], GAMMA ** (i[None, :] - i[:, None]).astype(np.float64), 0.0)
    decay = decay / np.sqrt(decay.sum(1))[None, :] / np.sqrt(D)
    c = np.zeros((P, C_END), np.float32)
    c[:, C_DECAY:C_DECAY + P] = decay.T
    c[:, C_TRI:C_TRI + P] = i[:, None] <= i[None, :]
    c[:, C_IDENT:C_IDENT + P] = np.eye(P)
    c[:, C_ONE] = 1.0
    c[:, C_TOK] = i
    c[:, C_ROW:C_ROW + P] = i[None, :]
    token = i[:, None] + P * np.arange(B)[None, :]
    c[:, C_CODE:C_CODE + TOPK * B] = np.concatenate([token + 1, -token - 1], axis=1)
    c[:, C_PREF:C_PREF + E] = E - np.arange(E)[None, :]
    h = np.zeros((P, H_END), np.float16)
    h[:, H_STRICT:H_STRICT + P] = i[:, None] < i[None, :]
    h[:, H_ONES:H_ONES + P] = 1.0
    h[:, H_ROW:H_ROW + P] = i[None, :]
    return c, h


def decoder_block(nc, x, xT, ctxt, ctxT, wvT, woT, freq_row, freq_col, routerT, weights, consts, halves, out):
    with ExitStack() as scope:
        def sb(name, shape, dt=F32):
            return scope.enter_context(nc.sbuf_tensor(name, shape, dt))

        def ps(name, shape, dt=F32):
            return scope.enter_context(nc.psum_tensor(name, shape, dt))

        def sem(name):
            return scope.enter_context(nc.semaphore(name))

        const = sb("const", [P, C_END])
        wv = sb("wv", [P, KC, D])
        wo = sb("wo", [P, KC, D])
        wr = sb("wr", [P, KC, E])
        frow = sb("frow", [P, D])
        fcol = sb("fcol", [P, KC])
        angle = sb("angle", [P, 2, D])
        turns = sb("turns", [P, 2, D])
        rem = sb("rem", [P, 2, D])
        rotor = sb("rotor", [P, 2, 2, D])

        keep = sb("keep", [P, PAIRS * 2 * D])
        x2_keep = keep[:].rearrange("p (j n) -> p j n", n=2 * D)
        w_in = [keep[:, s * W_END:(s + 1) * W_END] for s in range(2)]
        x_in = [keep[:, 2 * W_END + s * 2 * D:2 * W_END + (s + 1) * 2 * D].rearrange("p (q d) -> p q d", q=2)
                for s in range(2)]
        space = sb("space", [P, PAIRS * TOPK * 2 * D])
        y_all = space[:].rearrange("p (j c n) -> p j c n", j=PAIRS, c=TOPK)
        taken = [8 * 2 * D]

        def part_of_space(words, dt=F32):
            taken[0] += words
            return space[:, taken[0] - words:taken[0]].bitcast(dt)

        work = space[:, 0:8 * 2 * D].rearrange("p (a b n) -> p a b n", a=4, b=2)
        xT_in = [work[:, 0, s, :].rearrange("p (q k t) -> p q k t", q=2, k=KC) for s in range(2)]
        c_in = [work[:, 1, s, :].rearrange("p (q d) -> p q d", q=2) for s in range(2)]
        cT_in = [work[:, 2, s, :].rearrange("p (q k t) -> p q k t", q=2, k=KC) for s in range(2)]
        turned = work[:, 3, :, :].rearrange("p q (h d) -> p q h d", h=2)
        back = sb("back", [P, 2, 2, D])
        got = part_of_space(2 * KC * T).rearrange("p (q k t) -> p q k t", q=2, k=KC)
        r1 = sb("r1", [P, 2, D])
        st1 = sb("st1", [P, 2, 6])
        mv1 = sb("mv1", [P, 2, 2])
        sd1 = sb("sd1", [P, 2])
        rs1 = sb("rs1", [P, 2])
        x1 = [sb(f"x1_{s}", [P, 2, D]) for s in range(2)]
        x1T = sb("x1T", [P, 2, KC, T])
        att = sb("att", [P, 2, T])
        vabs = sb("vabs", [P, 2])
        vmax = sb("vmax", [P, 2])
        vinv = sb("vinv", [P, 2])
        cs = sb("cs", [P, 2, D])
        r2 = sb("r2", [P, 2, D])
        st2 = sb("st2", [P, 2, 6])
        mv2 = sb("mv2", [P, 2, 2])
        sd2 = sb("sd2", [P, 2])
        rs2 = sb("rs2", [P, 2])
        x2 = [sb(f"x2_{s}", [P, 2, D]) for s in range(2)]
        x2T = sb("x2T", [P, 2, KC, T])
        logits = sb("logits", [P, B, E])
        eps = sb("eps", [P, 1])
        unused = sb("unused", [P, 1])

        w_hi = sb("w_hi", [P, E, W_END], F32R)
        w_lo = sb("w_lo", [P, E, W_END], F32R)

        shift = [sb(f"shift{s}", [P, 2]) for s in range(2)]
        st_pair, mv_pair, sd_pair, rs_pair = [st1, st2], [mv1, mv2], [sd1, sd2], [rs1, rs2]

        half = sb("half", [P, H_END], F16)
        masked = sb("masked", [P, B, E])
        seen = [logits, masked]
        shifted = sb("shifted", [P, TOPK, B])
        expd = sb("expd", [P, TOPK, B])
        top = sb("top", [P, TOPK, B])
        ties = sb("ties", [P, B, E])
        key = sb("key", [P, B, E])
        kmax = sb("kmax", [P, B])
        pick = sb("pick", [P, TOPK, B, E])
        chosen = sb("chosen", [P, B + 1, E], F16)
        tsum = sb("tsum", [P, B])
        tinv = sb("tinv", [P, B])
        gate = sb("gate", [P, TOPK, B])
        need = sb("need", [P, E])
        upto = [sb(f"upto{n}", [P, 2 * E]) for n in range(4)]
        place = sb("place", [P, B, E])
        placed = sb("placed", [P, TOPK, B, E])
        slot = sb("slot", [P, TOPK * B])
        part = sb("part", [P, TOPK * B])
        tile_no = sb("tile_no", [P, TOPK * B])
        row_no = sb("row_no", [P, TOPK * B])
        row_hot = part_of_space(TOPK * B * P // 2, F16).rearrange("p (n r) -> p n r", r=P)
        tile_is = part_of_space(TOPK * B * TILES // 2, F16).rearrange("p (n r) -> p n r", r=TILES)
        tile_hot = part_of_space(TOPK * B * TILES // 2, F16).rearrange("p (n r) -> p n r", r=TILES)
        code = sb("code", [P, TILES])
        coded = sb("coded", [P, TILES])
        token = sb("token", [P, TILES])
        second = sb("second", [P, TILES])
        padding = sb("padding", [P, TILES])
        past = angle[:].rearrange("p h d -> p (h d)")[:, 0:TILES * E].rearrange("p (t e) -> p t e", e=E)
        expert = sb("expert", [P, TILES])
        gather_idx = sb("gather_idx", [P, TILES], I32)
        scatter_idx = sb("scatter_idx", [P, TILES], I32)
        gather_now = [sb(f"gather_now{s}", [P, 1], I32) for s in range(RING)]
        scatter_now = [sb(f"scatter_now{s}", [P, 1], I32) for s in range(RING)]
        expert_idx = sb("expert_idx", [P, TILES], I32)

        xs = [turns[:, 0, :], turns[:, 1, :], rem[:, 0, :]]
        xs_hi = [sb(f"xs_hi{s}", [P, KC, P], F32R) for s in range(RING)]
        xs_lo = [sb(f"xs_lo{s}", [P, KC, P], F32R) for s in range(RING)]
        silu, hid = cs[:, 0, :], cs[:, 1, :]
        hid_hi = [sb(f"hid_hi{s}", [P, KC, P], F32R) for s in range(RING)]
        hid_lo = [sb(f"hid_lo{s}", [P, KC, P], F32R) for s in range(RING)]
        ys = [x1T[:, 0, :, :].rearrange("p k t -> p (k t)"), x1T[:, 1, :, :].rearrange("p k t -> p (k t)"), x2T[:, 0, :, :].rearrange("p k t -> p (k t)")]

        x2_dram = nc.dram_tensor("x2_dram", (N, D), F32, kind="Internal").ap()
        y_dram = nc.dram_tensor("y_dram", (TOPK * N, D), F32, kind="Internal").ap()
        x2_pairs = x2_dram.rearrange("(j q t) d -> j t q d", q=2, t=T)
        y_pairs = y_dram.rearrange("(c j q t) d -> c j t q d", c=TOPK, q=2, t=T)

        p_v = ps("p_v", [P, 2, D])
        p_c = ps("p_c", [P, 2, 2, D])
        p_y = ps("p_y", [P, 2, D])
        p_t = ps("p_t", [P, 2, KC, T])
        p_s = ps("p_s", [P, 2 * D])
        p_a = ps("p_a", [P, 2, D])
        p_r = ps("p_r", [P, 2 * D])
        scores = p_s[:, 0:2 * T].rearrange("p (q s) -> p q s", q=2)
        rowsum = p_r[:, 0:2]
        plog = p_r[:, 64:64 + 2 * E].rearrange("p (q e) -> p q e", q=2)

        p_place = p_v[:].rearrange("p q d -> p (q d)")[:, 0:(B + 1) * E].rearrange("p (b e) -> p b e", e=E)
        p_inv = p_y[:].rearrange("p q d -> p (q d)")[:, 0:TILES]
        p_up = [p_v[:], p_c[:, 0, :, :], p_c[:, 1, :, :]]
        p_xt = p_y[:].rearrange("p q d -> p (q d)")[:, 0:D].rearrange("p (k t) -> p k t", k=KC)
        p_ht = p_t[:, 0, :, :]
        p_down = [p_s[:, 0:D], p_a[:, 0, :], p_r[:, 0:D]]

        tri = const[:, C_TRI:C_TRI + P]
        ident = const[:, C_IDENT:C_IDENT + P]
        decay = const[:, C_DECAY:C_DECAY + P].rearrange("p (a s) -> p a s", a=1).to_broadcast([P, 2, T])

        const_in, half_in, wv_in, proj_in, freq_in = (sem(n) for n in (
            "const_in", "half_in", "wv_in", "proj_in", "freq_in"))
        carried = sem("carried")
        w_ok = [sem(f"w_ok{s}") for s in range(2)]
        hi_ok, lo_ok = sem("hi_ok"), sem("lo_ok")
        gate_ok, row_no_ok, row_hot2_ok = sem("gate_ok"), sem("row_no_ok"), sem("row_hot2_ok")
        route, shift_ok, exp_ok, chosen_ok, place_ok = (sem(n) for n in (
            "route", "shift_ok", "exp_ok", "chosen_ok", "place_ok"))
        row_hot_ok, tile_hot_ok, inv_ok, index_ok, x2_saved = (sem(n) for n in (
            "row_hot_ok", "tile_hot_ok", "inv_ok", "index_ok", "x2_saved"))
        xs_ok = [sem(f"xs_ok{s}") for s in range(RING)]
        xt_ok, xhi_ok, xlo_ok, up_ok, silu_ok, hid_ok = (sem(n) for n in (
            "xt_ok", "xhi_ok", "xlo_ok", "up_ok", "silu_ok", "hid_ok"))
        ht_ok, hhi_ok, hlo_ok, down_ok, ys_ok = (sem(n) for n in (
            "ht_ok", "hhi_ok", "hlo_ok", "down_ok", "ys_ok"))
        gather_now_ok, scatter_now_ok = sem("gather_now_ok"), sem("scatter_now_ok")
        put_ok = [sem(f"put_ok{s}") for s in range(RING)]
        x2_back = sem("x2_back")
        y_back = [sem(f"y_back{j}") for j in range(PAIRS)]
        y_in_ok = sem("y_in_ok")
        weighed_ok, sum0_ok, r3_ok, st3_ok, mv3_ok, sd3_ok, rs3_ok, shift3_ok, res_ok = (sem(n) for n in (
            "weighed_ok", "sum0_ok", "r3_ok", "st3_ok", "mv3_ok", "sd3_ok", "rs3_ok", "shift3_ok", "res_ok"))
        out_ok = sem("out_ok")
        x_ok = [sem(f"x_ok{s}") for s in range(2)]
        xT_ok = [sem(f"xT_ok{s}") for s in range(2)]
        c_ok = [sem(f"c_ok{s}") for s in range(2)]
        cT_ok = [sem(f"cT_ok{s}") for s in range(2)]
        angle_ok, sine_ok, cosine_ok, rotor_ok = (sem(n) for n in ("angle_ok", "sine_ok", "cosine_ok", "rotor_ok"))
        eps_ok = sem("eps_ok")
        v_ok, turned_ok, sums_ok, back_ok, got_ok, y_ok = (sem(n) for n in (
            "v_ok", "turned_ok", "sums_ok", "back_ok", "got_ok", "y_ok"))
        r1_ok, st1_ok, mv1_ok, sd1_ok, rs1_ok, x1_ok = (sem(n) for n in (
            "r1_ok", "st1_ok", "mv1_ok", "sd1_ok", "rs1_ok", "x1_ok"))
        t1_ok, x1T_ok, sc_ok, att_ok, sum_ok, vabs_ok, vmax_ok, vinv_ok, cs_ok, av_ok = (sem(n) for n in (
            "t1_ok", "x1T_ok", "sc_ok", "att_ok", "sum_ok", "vabs_ok", "vmax_ok", "vinv_ok", "cs_ok", "av_ok"))
        r2_ok, st2_ok, mv2_ok, sd2_ok, rs2_ok, x2_ok = (sem(n) for n in (
            "r2_ok", "st2_ok", "mv2_ok", "sd2_ok", "rs2_ok", "x2_ok"))
        t2_ok, x2T_ok, lg_ok, logits_ok = (sem(n) for n in ("t2_ok", "x2T_ok", "lg_ok", "logits_ok"))
        x2_free = sem("x2_free")
        x2_out = [sem(f"x2_out{s}") for s in range(2)]

        def pipeline(engine, step, first=-1):
            def fixed(i):
                step(i, i % 2, lambda k: 0 <= i + k < PAIRS)
            for i in range(first, 2):
                fixed(i)
            with engine.Fori(1, PAIRS // 2 - 1) as half:
                step(2 * half, 0, lambda k: True)
                step(2 * half + 1, 1, lambda k: True)
            for i in range(PAIRS - 2, PAIRS + 2):
                fixed(i)

        def y_pair(i, c):
            return y_all[:, bass.ds(i, 1), c, :].rearrange("p a (q d) -> p (a q) d", q=2)

        def tile_pipeline(engine, step):
            def fixed(k):
                step(k, lambda d: ((k + d) % RING, (k + d) // RING), lambda d: 0 <= k + d < TILES)
            for k in range(-1, 2 * RING):
                fixed(k)
            last = RING * (TILES // RING - 2)
            with engine.Fori(0, (last - 2 * RING) // UNROLL) as trip:
                for u in range(2 * RING, 2 * RING + UNROLL):
                    step(UNROLL * trip + u, lambda d: ((u + d) % RING, UNROLL // RING * trip + (u + d) // RING),
                         lambda d: True)
            for k in range(last, TILES + 2):
                fixed(k)

        block = scope.enter_context(nc.Block())

        @block.sync
        def _(sp):
            def flat(v):
                names = "abcd"[:len(v.shape) - 1]
                return v.rearrange(f"p {' '.join(names)} -> p ({' '.join(names)})")

            def load(tile, src, ok, j, s):
                sp.dma_start(flat(tile[s]), src[bass.ds(j, 1), :, :].rearrange("a p n -> p (a n)")).then_inc(ok[s], 16)

            def step(i, s, has):
                if has(2):
                    if has(0):
                        sp.wait_ge(v_ok, i + 1)
                    load(xT_in, xT, xT_ok, i + 2, s)
                if has(1):
                    if has(-1):
                        sp.wait_ge(r1_ok, i)
                    load(x_in, x, x_ok, i + 1, 1 - s)
                    if has(-1):
                        sp.wait_ge(lo_ok, i)
                    load(w_in, weights, w_ok, i + 1, 1 - s)
                if has(-2):
                    sp.wait_ge(x2_ok, i - 1)
                    sp.dma_start(x2_pairs[bass.ds(i - 2, 1), :, :, :].rearrange("a t q d -> t (a q) d"),
                                 x2[s][:]).then_inc(x2_out[s], 16)
                if has(1):
                    if has(-1):
                        sp.wait_ge(sc_ok, i)
                    load(cT_in, ctxT, cT_ok, i + 1, 1 - s)
                    if has(-1):
                        sp.wait_ge(cs_ok, i)
                    load(c_in, ctxt, c_ok, i + 1, 1 - s)
                if has(-2):
                    sp.wait_ge(x2_out[s], 8 * (i - s))
                    sp.sem_inc(x2_free, 1)

            sp.sem_inc(x2_free, 2)
            sp.dma_start(frow[:], freq_row).then_inc(freq_in, 16)
            sp.dma_start(const[:], consts).then_inc(const_in, 16)
            sp.dma_start(fcol[:], freq_col).then_inc(freq_in, 16)
            load(xT_in, xT, xT_ok, 0, 0)
            sp.dma_start(wv[:], wvT).then_inc(wv_in, 16)
            step(-1, 1, lambda k: k in (1, 2))
            sp.dma_start(wo[:], woT).then_inc(proj_in, 16)
            sp.dma_start(wr[:], routerT).then_inc(proj_in, 16)
            sp.dma_start(half[:], halves).then_inc(half_in, 16)
            pipeline(sp, step, 0)
            sp.sem_inc(x2_saved, 1)
            sp.dma_start(x2_keep.rearrange("p j n -> p (j n)").rearrange("p (j q d) -> p (j q) d", q=2, d=D),
                         x2_dram.rearrange("(j t) d -> t j d", t=T)).then_inc(x2_back, 16)

            for s in range(RING):
                sp.wait_ge(put_ok[s], 16 * (TILES // RING))

            def load_rows(j):
                for c in range(TOPK):
                    sp.dma_start(y_all[:, j, c, :].rearrange("p (q d) -> p q d", q=2), y_pairs[c, j]).then_inc(
                        y_back[j], 16)

            for j in range(AHEAD):
                load_rows(j)
            for j in range(PAIRS):
                sp.wait_ge(y_back[j], 32)
                sp.sem_inc(y_in_ok, 1)
                if j + AHEAD < PAIRS:
                    load_rows(j + AHEAD)
            for j in range(PAIRS):
                sp.wait_ge(res_ok, j + 1)
                sp.dma_start(out[j], y_all[:, j, 1, :]).then_inc(out_ok, 16)
            sp.wait_ge(out_ok, 16 * PAIRS)

        @block.tensor
        def _(pe):
            pe.wait_ge(wv_in, 16)

            def values(q, s):
                for k in range(KC):
                    last = nc.tensor.matmul(p_v[:, q, :], xT_in[s][:, q, k, :], wv[:, k, :],
                                            start=(k == 0), stop=(k == KC - 1))
                return last

            def step(i, s, has):
                if isinstance(i, int) and i == 0:
                    pe.wait_ge(const_in, 16)
                    pe.wait_ge(proj_in, 32)
                if has(0):
                    pe.wait_ge(turned_ok, i + 1)
                    for q in range(2):
                        for h in range(2):
                            for k in range(KC):
                                last = nc.tensor.matmul(p_c[:, q, h, k * T:(k + 1) * T],
                                                        turned[:, q, h, k * P:(k + 1) * P], tri,
                                                        start=True, stop=True)
                    last.then_inc(sums_ok, 1)
                if has(-1):
                    pe.wait_ge(x1_ok, i)
                    for q in range(2):
                        for k in range(KC):
                            last = nc.tensor.transpose(p_t[:, q, k, :], x1[1 - s][:, q, k * P:(k + 1) * P], ident)
                    last.then_inc(t1_ok, 1)
                if has(1):
                    pe.wait_ge(xT_ok[1 - s], 8 * (i + s) + 16)
                    if has(0):
                        pe.wait_ge(turned_ok, i + 1)
                    values(0, 1 - s)
                if has(-1):
                    pe.wait_ge(cT_ok[1 - s], 8 * (i - 1 - (1 - s)) + 16)
                    pe.wait_ge(x1T_ok, i)
                    if has(-2):
                        pe.wait_ge(att_ok, i - 1)
                    for q in range(2):
                        for k in range(KC):
                            last = nc.tensor.matmul(scores[:, q, :], cT_in[1 - s][:, q, k, :], x1T[:, q, k, :],
                                                    start=(k == 0), stop=(k == KC - 1))
                    last.then_inc(sc_ok, 1)
                if has(1):
                    values(1, 1 - s).then_inc(v_ok, 1)
                if has(-1):
                    pe.wait_ge(att_ok, i)
                    for q in range(2):
                        last = nc.tensor.matmul(rowsum[:, q:q + 1], att[:, q, :], const[:, C_ONE:C_ONE + 1],
                                                start=True, stop=True)
                    last.then_inc(sum_ok, 1)
                if has(0):
                    pe.wait_ge(got_ok, i + 1)
                    for q in range(2):
                        for k in range(KC):
                            last = nc.tensor.matmul(p_y[:, q, :], got[:, q, k, :], wo[:, k, :],
                                                    start=(k == 0), stop=(k == KC - 1))
                    last.then_inc(y_ok, 1)
                if has(-2):
                    pe.wait_ge(x2_ok, i - 1)
                    if has(-1):
                        pe.wait_ge(x1T_ok, i)
                    for q in range(2):
                        for k in range(KC):
                            last = nc.tensor.transpose(p_t[:, q, k, :], x2[s][:, q, k * P:(k + 1) * P], ident)
                    last.then_inc(t2_ok, 1)
                if has(-1):
                    pe.wait_ge(cs_ok, i)
                    if has(-2):
                        pe.wait_ge(r2_ok, i - 1)
                    for q in range(2):
                        last = nc.tensor.matmul(p_a[:, q, :], att[:, q, :], cs[:, q, :], start=True, stop=True)
                    last.then_inc(av_ok, 1)
                if has(-2):
                    pe.wait_ge(x2T_ok, i - 1)
                    if has(-1):
                        pe.wait_ge(vabs_ok, i)
                    for q in range(2):
                        for k in range(KC):
                            last = nc.tensor.matmul(plog[:, q, :], x2T[:, q, k, :], wr[:, k, :],
                                                    start=(k == 0), stop=(k == KC - 1))
                    last.then_inc(lg_ok, 1)

            pipeline(pe, step)

            pe.wait_ge(half_in, 16)
            pe.wait_ge(chosen_ok, 2)
            nc.tensor.matmul(p_place, half[:, H_STRICT:H_STRICT + P], chosen[:], start=True, stop=True, skip_group_check=True)
            for b in range(B):
                last = nc.tensor.matmul(p_place[:, b + 1:, :], half[:, H_ONES:H_ONES + P],
                                        chosen[:, b:b + 1, :].to_broadcast([P, B - b, E]),
                                        start=False, stop=True, skip_group_check=True)
            last.then_inc(place_ok, 1)
            pe.wait_ge(tile_hot_ok, 2)
            for n in range(TOPK * B):
                pe.wait_ge(*((row_hot2_ok, n // 3 + 1) if n % 3 == 2 else (row_hot_ok, n - n // 3 + 1)))
                last = nc.tensor.matmul(p_inv, row_hot[:, n, :], tile_hot[:, n, :],
                                        start=(n == 0), stop=(n == TOPK * B - 1))
            last.then_inc(inv_ok, 1)
            pe.wait_ge(index_ok, 1)

            def split_product(dst, lhs_hi, lhs_lo, col, width, start):
                n = 0
                for lhs, w in ((lhs_hi, w_hi), (lhs_hi, w_lo), (lhs_lo, w_hi)):
                    for k in range(KC):
                        last = nc.tensor.matmul(dst, lhs[:, k, :],
                                                w[:].rearrange("p e n -> p (e n)")[:, bass.ds(start + col + k * width, width)],
                                                start=(n == 0), stop=(n == 3 * KC - 1))
                        n += 1
                return last

            count = [0]

            def weights_at(k, name):
                count[0] += 1
                register = pe.alloc_register(f"{name}{count[0]}")
                pe.reg_load(register, expert_idx[0:1, bass.ds(k, 1)])
                return pe.snap(register, donate=True, min_val=0, max_val=(E - 1) * W_END)

            def tile(k, at, has):
                if has(-2):
                    down_at = weights_at(k - 2, "down_at")
                if has(0):
                    up_at = weights_at(k, "up_at")
                if has(1):
                    s, used = at(1)
                    pe.wait_ge(xs_ok[s], 16 * used + 16)
                    if has(0):
                        pe.wait_ge(xlo_ok, k + 1)
                    for c in range(KC):
                        last = nc.tensor.transpose(p_xt[:, c, :], xs[s][:, c * P:(c + 1) * P], ident)
                    last.then_inc(xt_ok, 1)
                if has(0):
                    s, _ = at(0)
                    pe.wait_ge(xlo_ok, k + 1)
                    if has(-3):
                        pe.wait_ge(hid_ok, k - 2)
                    split_product(p_up[s], xs_hi[s], xs_lo[s], W_UP, 2 * DH, up_at).then_inc(up_ok, 1)
                if has(-1):
                    pe.wait_ge(hid_ok, k)
                    if has(-2):
                        pe.wait_ge(hlo_ok, k - 1)
                    for c in range(KC):
                        last = nc.tensor.transpose(p_ht[:, c, :], hid[:, c * P:(c + 1) * P], ident)
                    last.then_inc(ht_ok, 1)
                if has(-2):
                    s, _ = at(-2)
                    pe.wait_ge(hlo_ok, k - 1)
                    if has(-5):
                        pe.wait_ge(ys_ok, k - 4)
                    split_product(p_down[s], hid_hi[s], hid_lo[s], W_DOWN, D, down_at).then_inc(down_ok, 1)

            tile_pipeline(pe, tile)

        @block.vector
        def _(dve):
            dve.wait_ge(const_in, 16)
            dve.wait_ge(freq_in, 32)
            nc.vector.memset(eps[:], EPS).then_inc(eps_ok, 1)
            tok = const[:, C_TOK:C_TOK + 1]
            count = [0]

            def after(ins):
                count[0] += 1
                ins.then_inc(angle_ok, 1)
                dve.wait_ge(angle_ok, count[0])

            def angles(h):
                a, t, r = angle[:, h, :], turns[:, h, :], rem[:, h, :]
                if h == 0:
                    after(nc.vector.tensor_scalar(a, frow[:], tok, None, ALU.mult))
                else:
                    for k in range(KC):
                        after(nc.vector.tensor_scalar(angle[:, 1, k * T:(k + 1) * T], const[:, C_ROW:C_ROW + P],
                                                      fcol[:, k:k + 1], None, ALU.mult))
                after(nc.vector.tensor_scalar(t, a, 1.0 / TWO_PI, ROUND, ALU.mult, ALU.add))
                after(nc.vector.tensor_scalar(r, t, -ROUND, None, ALU.add))
                after(nc.vector.scalar_tensor_tensor(t, r, -TURN_HI, a, ALU.mult, ALU.add))

            def arguments(h):
                a, t, r = angle[:, h, :], turns[:, h, :], rem[:, h, :]
                after(nc.vector.scalar_tensor_tensor(a, r, -TURN_MID, t, ALU.mult, ALU.add))
                after(nc.vector.scalar_tensor_tensor(t, r, -TURN_LO, a, ALU.mult, ALU.add))
                nc.vector.tensor_scalar(a, t, SIN_MAX, -SIN_MAX, ALU.min, ALU.max).then_inc(sine_ok, 1)
                dve.wait_ge(sine_ok, h + 1)
                after(nc.vector.scalar_tensor_tensor(t, a, -1.0, a, ALU.mult, ALU.min))
                nc.vector.tensor_scalar(r, t, np.pi / 2, None, ALU.add).then_inc(cosine_ok, 1)

            angles(0)
            arguments(0)
            angles(1)

            def statistics(j, src, st, mv, r_ok, st_ok, mv_ok):
                dve.wait_ge(r_ok, j + 1)
                for q in range(2):
                    nc.vector.bn_stats(st[:, q, :], src[:, q, :]).then_inc(st_ok, 1)
                dve.wait_ge(st_ok, 2 * j + 2)
                dve.sem_inc(carried, 1)
                for q in range(2):
                    nc.vector.bn_aggr(mv[:, q, :], st[:, q, :]).then_inc(mv_ok, 1)

            def normalise(j, src, mv, sd, rs, dst, sd_ok, rs_ok, dst_ok):
                dve.wait_ge(sd_ok, j + 1)
                nc.vector.reciprocal(rs[:], sd[:]).then_inc(rs_ok, 1)
                dve.wait_ge(rs_ok, j + 1)
                for q in range(2):
                    last = nc.vector.tensor_scalar(dst[:, q, :], src[:, q, :], mv[:, q, 0:1], rs[:, q:q + 1],
                                                   ALU.subtract, ALU.mult)
                last.then_inc(dst_ok, 1)

            def turn(j):
                dve.wait_ge(v_ok, j + 1)
                for q in range(2):
                    last = nc.vector.tensor_tensor(
                        turned[:, q, :, :], p_v[:, q:q + 1, :].to_broadcast([P, 2, D]), rotor[:, 0, :, :], ALU.mult)
                last.then_inc(turned_ok, 1)

            def step(i, s, has):
                if has(-2):
                    dve.wait_ge(av_ok, i - 1)
                    nc.vector.tensor_tensor(r2[:], p_a[:], x1[s][:], ALU.add).then_inc(r2_ok, 1)
                if has(-1):
                    normalise(i - 1, r1, mv1, sd1, rs1, x1[1 - s], sd1_ok, rs1_ok, x1_ok)
                if has(0):
                    dve.wait_ge(sums_ok, i + 1)
                    if isinstance(i, int) and i == 0:
                        dve.wait_ge(rotor_ok, 4)
                    if has(-1):
                        dve.wait_ge(got_ok, i)
                    for q in range(2):
                        last = nc.vector.tensor_tensor(back[:, q, :, :], p_c[:, q, :, :], rotor[:, 1, :, :], ALU.mult)
                    last.then_inc(back_ok, 1)
                if has(-2):
                    statistics(i - 2, r2, st2, mv2, r2_ok, st2_ok, mv2_ok)
                if has(-1):
                    dve.wait_ge(sc_ok, i)
                    nc.vector.tensor_tensor(att[:], scores, decay, ALU.mult).then_inc(att_ok, 1)
                if has(-2):
                    dve.wait_ge(x2_free, i - 1)
                    normalise(i - 2, r2, mv2, sd2, rs2, x2[s], sd2_ok, rs2_ok, x2_ok)
                if has(-1):
                    dve.wait_ge(vabs_ok, i)
                    nc.vector.tensor_scalar(vmax[:], vabs[:], 1.0, None, ALU.max).then_inc(vmax_ok, 1)
                    dve.wait_ge(vmax_ok, i)
                    nc.vector.reciprocal(vinv[:], vmax[:]).then_inc(vinv_ok, 1)
                if has(1):
                    if isinstance(i, int) and i == -1:
                        dve.wait_ge(rotor_ok, 2)
                    turn(i + 1)
                    if isinstance(i, int) and i == -1:
                        arguments(1)
                if has(0):
                    dve.wait_ge(y_ok, i + 1)
                    dve.wait_ge(x_ok[s], 8 * (i - s) + 16)
                    nc.vector.tensor_tensor(r1[:], p_y[:], x_in[s], ALU.add).then_inc(r1_ok, 1)
                    statistics(i, r1, st1, mv1, r1_ok, st1_ok, mv1_ok)

            pipeline(dve, step)

            count = [0]

            def link(ins):
                count[0] += 1
                ins.then_inc(route, 1)
                dve.wait_ge(route, count[0])

            def over_e(v):
                return v.unsqueeze(2).to_broadcast([P, B, E])

            nc.vector.memset(chosen[:, B, :], 0.0).then_inc(chosen_ok, 1)
            for n in range(4):
                link(nc.vector.memset(upto[n][:], 0.0))
            dve.wait_ge(logits_ok, PAIRS)
            for c in range(TOPK):
                link(nc.vector.tensor_reduce(top[:, c, :], seen[c][:], AX_X, ALU.max))
                link(nc.vector.tensor_tensor(ties[:], seen[c][:], over_e(top[:, c, :]), ALU.is_equal))
                pref = const[:, C_PREF:C_PREF + E].unsqueeze(1).to_broadcast([P, B, E])
                link(nc.vector.tensor_tensor(key[:], ties[:], pref, ALU.mult))
                link(nc.vector.tensor_reduce(kmax[:], key[:], AX_X, ALU.max))
                link(nc.vector.tensor_tensor(pick[:, c, :, :], key[:], over_e(kmax[:]), ALU.is_equal))
                if c == 0:
                    link(nc.vector.scalar_tensor_tensor(masked[:], pick[:, 0, :, :], -MASKED, logits[:], ALU.mult, ALU.add))
            nc.vector.tensor_tensor(chosen[:, 0:B, :], pick[:, 0, :, :], pick[:, 1, :, :], ALU.add).then_inc(chosen_ok, 1)
            nc.vector.tensor_tensor(shifted[:], top[:], top[:, 0:1, :].to_broadcast([P, TOPK, B]), ALU.subtract).then_inc(shift_ok, 1)
            dve.wait_ge(place_ok, 1)
            link(nc.vector.tensor_scalar(need[:], p_place[:, B, :], HALF, 1.0 / P, ALU.add, ALU.mult))
            link(nc.vector.tensor_scalar(upto[0][:, E:], need[:], ROUND, -ROUND, ALU.add, ALU.add))
            for n in range(3):
                by = 2 ** n
                link(nc.vector.tensor_tensor(upto[n + 1][:, E:], upto[n][:, E:], upto[n][:, E - by:2 * E - by], ALU.add))
            base = upto[3][:, E - 1:2 * E - 1].unsqueeze(1).to_broadcast([P, B, E])
            link(nc.vector.scalar_tensor_tensor(place[:], base, float(P), p_place[:, 0:B, :], ALU.mult, ALU.add))
            link(nc.vector.tensor_tensor(placed[:], pick[:], place[:].unsqueeze(1).to_broadcast([P, TOPK, B, E]), ALU.mult))
            link(nc.vector.tensor_reduce(slot[:], placed[:].rearrange("p c b e -> p (c b) e"), AX_X, ALU.add))
            link(nc.vector.tensor_scalar(part[:], slot[:], -HALF, 1.0 / P, ALU.add, ALU.mult))
            link(nc.vector.tensor_scalar(tile_no[:], part[:], ROUND, -ROUND, ALU.add, ALU.add))
            nc.vector.scalar_tensor_tensor(row_no[:], tile_no[:], -float(P), slot[:], ALU.mult, ALU.add).then_inc(row_no_ok, 1)
            dve.wait_ge(row_no_ok, 1)
            tiles_row = const[:, C_ROW:C_ROW + TILES].unsqueeze(1).to_broadcast([P, TOPK * B, TILES])
            nc.vector.tensor_tensor(tile_is, tiles_row, tile_no[:].unsqueeze(2).to_broadcast([P, TOPK * B, TILES]),
                                    ALU.is_equal).then_inc(tile_hot_ok, 1)
            dve.wait_ge(tile_hot_ok, 1)
            codes = const[:, C_CODE:C_CODE + TOPK * B].unsqueeze(2).to_broadcast([P, TOPK * B, TILES])
            nc.vector.tensor_tensor(tile_hot, tile_is, codes, ALU.mult).then_inc(tile_hot_ok, 1)
            for n in range(TOPK * B):
                if n % 3 != 2:
                    nc.vector.tensor_scalar(row_hot[:, n, :], half[:, H_ROW:H_ROW + P], row_no[:, n:n + 1], None,
                                            ALU.is_equal).then_inc(row_hot_ok, 1)
            dve.wait_ge(inv_ok, 1)
            link(nc.vector.tensor_copy(code[:], p_inv))
            link(nc.vector.scalar_tensor_tensor(coded[:], code[:], -1.0, code[:], ALU.mult, ALU.max))
            link(nc.vector.tensor_scalar(token[:], coded[:], -1.0, 0.0, ALU.add, ALU.max))
            link(nc.vector.tensor_copy(gather_idx[:], token[:]))
            for k in range(RING):
                nc.vector.tensor_copy(gather_now[k][:], gather_idx[:, k:k + 1]).then_inc(gather_now_ok, 1)
            link(nc.vector.tensor_tensor(past, const[:, C_ROW:C_ROW + TILES].unsqueeze(2).to_broadcast([P, TILES, E]),
                                         upto[3][:, E:].unsqueeze(1).to_broadcast([P, TILES, E]), ALU.is_ge))
            link(nc.vector.tensor_reduce(expert[:], past, AX_X, ALU.add))
            nc.vector.tensor_scalar(expert_idx[:], expert[:], float(E - 1), float(W_END), ALU.min, ALU.mult).then_inc(index_ok, 1)
            nc.vector.tensor_scalar(second[:], code[:], 0.0, float(N), ALU.is_lt, ALU.mult).then_inc(index_ok, 1)
            nc.vector.tensor_scalar(padding[:], code[:], 0.0, float(SKIP), ALU.is_equal, ALU.mult).then_inc(index_ok, 1)
            dve.wait_ge(index_ok, 3)
            link(nc.vector.tensor_tensor(coded[:], token[:], second[:], ALU.add))
            link(nc.vector.tensor_tensor(scatter_idx[:], coded[:], padding[:], ALU.add))
            dve.wait_ge(exp_ok, 1)
            link(nc.vector.tensor_tensor(tsum[:], expd[:, 0, :], expd[:, 1, :], ALU.add))
            link(nc.vector.reciprocal(tinv[:], tsum[:]))
            nc.vector.tensor_tensor(gate[:], expd[:], tinv[:].unsqueeze(1).to_broadcast([P, TOPK, B]), ALU.mult).then_inc(gate_ok, 1)

            def tile(k, at, has):
                if has(1):
                    s, _ = at(1)
                    dve.wait_ge(xhi_ok, k + 2)
                    nc.vector.tensor_tensor(xs_lo[s][:], p_xt, xs_hi[s][:].bitcast(F32), ALU.subtract).then_inc(xlo_ok, 1)
                if has(4):
                    s, _ = at(1)
                    nc.vector.tensor_copy(gather_now[s][:], gather_idx[:, bass.ds(k + 4, 1)]).then_inc(gather_now_ok, 1)
                if has(0):
                    s, _ = at(0)
                    dve.wait_ge(silu_ok, k + 1)
                    if has(-1):
                        dve.wait_ge(ht_ok, k)
                    up_rows = p_up[s].rearrange("p q d -> p (q d)")[:, DH:2 * DH]
                    nc.vector.tensor_tensor(hid, up_rows, silu, ALU.mult).then_inc(hid_ok, 1)
                if has(-1):
                    s, _ = at(-1)
                    dve.wait_ge(hhi_ok, k)
                    nc.vector.tensor_tensor(hid_lo[s][:], p_ht, hid_hi[s][:].bitcast(F32), ALU.subtract).then_inc(hlo_ok, 1)
                if has(-2):
                    s, _ = at(-2)
                    if has(-5):
                        dve.wait_ge(put_ok[s], 16 * at(-2)[1])
                    nc.vector.tensor_copy(scatter_now[s][:], scatter_idx[:, bass.ds(k - 2, 1)]).then_inc(scatter_now_ok, 1)

            tile_pipeline(dve, tile)

            def finish(i, s, has):
                if has(0):
                    dve.wait_ge(sum0_ok, i + 1)
                    for q in range(2):
                        last = nc.vector.scalar_tensor_tensor(
                            y_pair(i, 0)[:, q, :], y_pair(i, 1)[:, q, :], gate[:, 1, bass.ds(2 * i + q, 1)],
                            y_pair(i, 0)[:, q, :], ALU.mult, ALU.add)
                    last.then_inc(r3_ok, 1)
                if has(-1):
                    dve.wait_ge(sd3_ok, i)
                    nc.vector.reciprocal(rs_pair[1 - s][:], sd_pair[1 - s][:]).then_inc(rs3_ok, 1)
                if has(0):
                    dve.wait_ge(r3_ok, i + 1)
                    dve.sem_inc(carried, 1)
                    for q in range(2):
                        nc.vector.bn_stats(st_pair[s][:, q, :], y_pair(i, 0)[:, q, :]).then_inc(st3_ok, 1)
                if has(-1):
                    dve.wait_ge(rs3_ok, i)
                    nc.vector.scalar_tensor_tensor(shift[1 - s][:], mv_pair[1 - s][:, :, 0], -1.0, rs_pair[1 - s][:],
                                                   ALU.mult, ALU.mult).then_inc(shift3_ok, 1)
                if has(0):
                    dve.wait_ge(st3_ok, 2 * i + 2)
                    dve.sem_inc(carried, 1)
                    for q in range(2):
                        nc.vector.bn_aggr(mv_pair[s][:, q, :], st_pair[s][:, q, :]).then_inc(mv3_ok, 1)

            pipeline(dve, finish, 0)

        @block.scalar
        def _(act):
            for h in range(2):
                act.wait_ge(sine_ok, h + 1)
                nc.scalar.activation(rotor[:, h, 1, :], angle[:, h, :], ACT.Sin).then_inc(rotor_ok, 1)
                act.wait_ge(cosine_ok, h + 1)
                nc.scalar.activation(rotor[:, h, 0, :], rem[:, h, :], ACT.Sin).then_inc(rotor_ok, 1)
            act.wait_ge(eps_ok, 1)

            def step(i, s, has):
                if has(-1):
                    act.wait_ge(mv1_ok, 2 * i)
                    nc.scalar.activation(sd1[:], mv1[:, :, 1], ACT.Sqrt, bias=eps[:]).then_inc(sd1_ok, 1)
                    act.wait_ge(t1_ok, i)
                    nc.scalar.activation(x1T[:], p_t[:], ACT.Copy).then_inc(x1T_ok, 1)
                if has(-2):
                    act.wait_ge(mv2_ok, 2 * i - 2)
                    nc.scalar.activation(sd2[:], mv2[:, :, 1], ACT.Sqrt, bias=eps[:]).then_inc(sd2_ok, 1)
                if has(-1):
                    act.wait_ge(sum_ok, i)
                    nc.scalar.activation(vabs[:], rowsum, ACT.Abs).then_inc(vabs_ok, 1)
                if has(0):
                    act.wait_ge(w_ok[s], 8 * (i - s) + 16)
                    nc.scalar.activation(w_hi[:, bass.ds(i, 1), :].rearrange("p a n -> p (a n)"), w_in[s],
                                         ACT.Copy).then_inc(hi_ok, 1)
                if has(-2):
                    act.wait_ge(t2_ok, i - 1)
                    nc.scalar.activation(x2T[:], p_t[:], ACT.Copy).then_inc(x2T_ok, 1)
                    act.wait_ge(lg_ok, i - 1)
                    nc.scalar.activation(logits[:, bass.ds(2 * (i - 2), 2), :], plog, ACT.Copy).then_inc(logits_ok, 1)

            pipeline(act, step)

            act.wait_ge(shift_ok, 1)
            nc.scalar.activation(expd[:], shifted[:], ACT.Exp).then_inc(exp_ok, 1)
            nc.scalar.activation(unused[:], eps[:], ACT.Silu)

            def tile(k, at, has):
                if has(1):
                    s, _ = at(1)
                    act.wait_ge(xt_ok, k + 2)
                    nc.scalar.activation(xs_hi[s][:], p_xt, ACT.Copy).then_inc(xhi_ok, 1)
                if has(0):
                    s, _ = at(0)
                    act.wait_ge(up_ok, k + 1)
                    if has(-1):
                        act.wait_ge(hid_ok, k)
                    gate_rows = p_up[s].rearrange("p q d -> p (q d)")[:, 0:DH]
                    nc.scalar.activation(silu, gate_rows, ACT.Silu).then_inc(silu_ok, 1)
                if has(-1):
                    s, _ = at(-1)
                    act.wait_ge(ht_ok, k)
                    if has(-4):
                        act.wait_ge(down_ok, k - 3)
                    nc.scalar.activation(hid_hi[s][:], p_ht, ACT.Copy).then_inc(hhi_ok, 1)
                if has(-2):
                    s, used = at(-2)
                    act.wait_ge(down_ok, k - 1)
                    if has(-5):
                        act.wait_ge(put_ok[s], 16 * used)
                    nc.scalar.activation(ys[s], p_down[s], ACT.Copy).then_inc(ys_ok, 1)

            tile_pipeline(act, tile)

            act.wait_ge(gate_ok, 1)
            nc.scalar.activation(unused[:], eps[:], ACT.Sqrt)

            def weigh(j):
                act.wait_ge(y_in_ok, j + 1)
                for q in range(2):
                    nc.scalar.activation(y_pair(j, 0)[:, q, :], y_pair(j, 0)[:, q, :], ACT.Copy,
                                         scale=gate[:, 0, bass.ds(2 * j + q, 1)]).then_inc(weighed_ok, 1)

            def finish(i, s, has):
                if isinstance(i, int) and i == -1:
                    weigh(0)
                if has(0):
                    act.wait_ge(mv3_ok, 2 * i + 2)
                    nc.scalar.activation(sd_pair[s][:], mv_pair[s][:, :, 1], ACT.Sqrt, bias=eps[:]).then_inc(sd3_ok, 1)
                if has(2):
                    weigh(i + 2)
                if has(-1):
                    act.wait_ge(shift3_ok, i)
                    for q in range(2):
                        last = nc.scalar.activation(y_pair(i - 1, 1)[:, q, :], y_pair(i - 1, 0)[:, q, :], ACT.Identity,
                                                    scale=rs_pair[1 - s][:, q:q + 1], bias=shift[1 - s][:, q:q + 1])
                    last.then_inc(res_ok, 1)

            pipeline(act, finish)

        @block.gpsimd
        def _(pool):
            def step(i, s, has):
                if has(0):
                    pool.wait_ge(back_ok, i + 1)
                    if has(-1):
                        pool.wait_ge(y_ok, i)
                    nc.gpsimd.tensor_tensor(got, back[:, :, 0, :].rearrange("p q (k t) -> p q k t", k=KC),
                                            back[:, :, 1, :].rearrange("p q (k t) -> p q k t", k=KC), ALU.add).then_inc(got_ok, 1)
                if has(-1):
                    pool.wait_ge(c_ok[1 - s], 8 * (i - 1 - (1 - s)) + 16)
                    pool.wait_ge(vinv_ok, i)
                    if has(-2):
                        pool.wait_ge(av_ok, i - 1)
                    for q in range(2):
                        last = nc.gpsimd.tensor_tensor(cs[:, q, :], c_in[1 - s][:, q, :], vinv[:, q:q + 1].to_broadcast([P, D]), ALU.mult)
                    last.then_inc(cs_ok, 1)

                if has(0):
                    pool.wait_ge(hi_ok, i + 1)
                    nc.gpsimd.tensor_tensor(w_lo[:, bass.ds(i, 1), :].rearrange("p a n -> p (a n)"), w_in[s],
                                            w_hi[:, bass.ds(i, 1), :].rearrange("p a n -> p (a n)").bitcast(F32),
                                            ALU.subtract).then_inc(lo_ok, 1)

            pipeline(pool, step)

            for n in range(2, TOPK * B, 3):
                if n == 2:
                    pool.wait_ge(half_in, 16)
                    pool.wait_ge(row_no_ok, 1)
                nc.gpsimd.tensor_scalar(row_hot[:, n, :], half[:, H_ROW:H_ROW + P], row_no[:, n:n + 1], None,
                                        ALU.is_equal).then_inc(row_hot2_ok, 1)

            def gather(s):
                nc.gpsimd.indirect_dma_start(xs[s], None, x2_dram,
                                             bass.IndirectOffsetOnAxis(ap=gather_now[s][:], axis=0)).then_inc(xs_ok[s], 16)

            pool.wait_ge(x2_saved, 1)
            for k in range(RING):
                pool.wait_ge(gather_now_ok, k + 1)
                gather(k)

            def tile(k, at, has):
                if has(4):
                    s, _ = at(1)
                    pool.wait_ge(gather_now_ok, k + 5)
                    pool.sem_inc(carried, 1)
                    gather(s)
                if has(-2):
                    s, _ = at(-2)
                    pool.wait_ge(scatter_now_ok, k - 1)
                    pool.wait_ge(ys_ok, k - 1)
                    pool.sem_inc(carried, 1)
                    nc.gpsimd.indirect_dma_start(
                        y_dram, bass.IndirectOffsetOnAxis(ap=scatter_now[s][:], axis=0),
                        ys[s], None, bounds_check=TOPK * N - 1, oob_is_err=False).then_inc(put_ok[s], 16)

            tile_pipeline(pool, tile)

            pool.wait_ge(x2_back, 16)

            def finish(i, s, has):
                if has(1):
                    pool.wait_ge(weighed_ok, 2 * i + 4)
                    nc.gpsimd.tensor_tensor(y_pair(i + 1, 0), y_pair(i + 1, 0),
                                            x2_keep[:, bass.ds(i + 1, 1), :].rearrange("p a (q d) -> p (a q) d", q=2),
                                            ALU.add).then_inc(sum0_ok, 1)

            pipeline(pool, finish)


def kernel(**inputs):
    import numpy as _np
    import concourse.bacc as _bacc
    from concourse import mybir as _mybir
    from concourse.bass_utils import run_bass_kernel_spmd as _run

    a = {k: _np.asarray(v) for k, v in inputs.items()}

    def rows(v):
        return v.reshape(PAIRS, 2, T, D).transpose(0, 2, 1, 3).reshape(PAIRS, P, 2 * D)

    def columns(v):
        return v.reshape(PAIRS, 2, T, KC, P).transpose(0, 4, 1, 3, 2).reshape(PAIRS, P, 2 * D)

    def chunked(v):
        return v.reshape(KC, P, v.shape[-1]).transpose(1, 0, 2)

    consts, halves = shape_constants()
    freqs = a["L0_attn_freqs"]
    arrays = {
        "x": rows(a["x"]), "xT": columns(a["x"]),
        "ctxt": rows(a["ctx_1024"]), "ctxT": columns(a["ctx_1024"]),
        "wvT": chunked(a["L0_attn_Wv"].T), "woT": chunked(a["L0_attn_Wo"].T),
        "freq_row": _np.broadcast_to(freqs, (P, D)), "freq_col": freqs.reshape(KC, P).T,
        "routerT": chunked(a["L0_ffn_router_w"].T),
        "weights": _np.concatenate([
            a["L0_ffn_up_proj"].reshape(E, KC, P, 2 * DH).transpose(0, 2, 1, 3).reshape(E, P, W_DOWN),
            a["L0_ffn_down_proj"].reshape(E, KC, P, D).transpose(0, 2, 1, 3).reshape(E, P, KC * D)], axis=2),
        "consts": consts, "halves": halves,
    }
    arrays = {k: _np.ascontiguousarray(v) for k, v in arrays.items()}
    nc = _bacc.Bacc("TRN2", target_bir_lowering=False, num_devices=1)
    args = {k: nc.dram_tensor(f"in_{k}", v.shape, _mybir.dt.from_np(v.dtype), kind="ExternalInput").ap()
            for k, v in arrays.items()}
    out = nc.dram_tensor("out_0", (PAIRS, P, 2 * D), _mybir.dt.float32, kind="ExternalOutput").ap()
    decoder_block(nc, out=out, **args)
    r = _run(nc, [{f"in_{k}": v for k, v in arrays.items()}], core_ids=[0])
    got = r.results[0]["out_0"]
    return got.reshape(PAIRS, P, 2, D).transpose(0, 2, 1, 3).reshape(B, T, D)
```

```python
from contextlib import ExitStack

import numpy as np

import concourse.bass as bass
from concourse import mybir

ALU = mybir.AluOpType
ACT = mybir.ActivationFunctionType
AX_X = mybir.AxisListType.X
F32 = mybir.dt.float32
F32R = mybir.dt.float32r
F16 = mybir.dt.float16
I32 = mybir.dt.int32

P = 128
B, T, D = 16, 128, 256
KC = D // P
PAIRS = B // 2
E, DH = 8, 256
TOPK = 2
N = B * T
TILES = (N * TOPK + E * (P - 1)) // P
EPS = 1e-5
GAMMA = 0.96875
MASKED = 1e30
SKIP = 4 * N

ROUND = 12582912.0
TWO_PI = 2.0 * np.pi
TURN_HI = 6.28125
TURN_MID = float(np.float32(np.round((TWO_PI - TURN_HI) * 2.0 ** 21) / 2.0 ** 21))
TURN_LO = float(np.float32(TWO_PI - TURN_HI - TURN_MID))
SIN_MAX = 3.1415925

DVE_ROWS, POOL_ROWS, ACT_ROWS = range(0, 11), range(11, 20), range(20, TOPK * B)

C_DECAY, C_TRI, C_IDENT, C_ONE, C_ROW = 0, P, 2 * P, 3 * P, 3 * P + 1
C_PREF = C_ROW + P
C_END = C_PREF + E
H_STRICT, H_ONES, H_ROW, H_CODE = 0, P, 2 * P, 3 * P
H_END = H_CODE + TOPK * B
W_UP, W_DOWN = 0, KC * 2 * DH
W_END = W_DOWN + KC * D
LATE = 4
FILL = ((0, 3, 2, 0, 0), (7, 4, 3, 5, 0), (15, 0, 0, 0, 3))
AHEAD = 3
RING = 3
UNROLL = 3 * RING
HALF = 63.5


def shape_constants():
    i = np.arange(P)
    decay = np.where(i[:, None] >= i[None, :], GAMMA ** (i[None, :] - i[:, None]).astype(np.float64), 0.0)
    decay = decay / np.sqrt(decay.sum(1))[None, :] / np.sqrt(D)
    c = np.zeros((P, C_END), np.float32)
    c[:, C_DECAY:C_DECAY + P] = decay.T
    c[:, C_TRI:C_TRI + P] = i[:, None] <= i[None, :]
    c[:, C_IDENT:C_IDENT + P] = np.eye(P)
    c[:, C_ONE] = 1.0
    c[:, C_ROW:C_ROW + P] = i[None, :]
    c[:, C_PREF:C_PREF + E] = E - np.arange(E)[None, :]
    h = np.zeros((P, H_END), np.float16)
    h[:, H_STRICT:H_STRICT + P] = i[:, None] < i[None, :]
    h[:, H_ONES:H_ONES + P] = 1.0
    h[:, H_ROW:H_ROW + P] = i[None, :]
    token = i[:, None] + P * np.arange(B)[None, :]
    h[:, H_CODE:H_CODE + TOPK * B] = np.concatenate([token + 1, -token - 1], axis=1)
    return c, h


def decoder_block(nc, x, xT, ctxt, ctxT, wvT, woT, freq, routerT, weights, consts, halves, out):
    with ExitStack() as scope:
        def sb(name, shape, dt=F32):
            return scope.enter_context(nc.sbuf_tensor(name, shape, dt))

        def ps(name, shape, dt=F32):
            return scope.enter_context(nc.psum_tensor(name, shape, dt))

        def sem(name):
            return scope.enter_context(nc.semaphore(name))

        const = sb("const", [P, C_END])
        wv = sb("wv", [P, KC, D])
        wo = sb("wo", [P, KC, D])
        wr = sb("wr", [P, KC, E])
        freqs = sb("freqs", [P, D + KC + 1])
        frow, fcol, tok = freqs[:, 0:D], freqs[:, D:D + KC], freqs[:, D + KC:]
        angle = sb("angle", [P, 2, D])
        turns = sb("turns", [P, 2, D])
        rem = sb("rem", [P, 2, D])
        rotor = sb("rotor", [P, 2, 2, D])

        keep = sb("keep", [P, PAIRS * 2 * D])
        x2_keep = keep[:].rearrange("p (j n) -> p j n", n=2 * D)
        w_in = [keep[:, s * W_END:(s + 1) * W_END] for s in range(2)]
        x_in = [keep[:, 2 * W_END + s * 2 * D:2 * W_END + (s + 1) * 2 * D].rearrange("p (q d) -> p q d", q=2)
                for s in range(2)]
        space = sb("space", [P, PAIRS * TOPK * 2 * D])
        y_all = space[:].rearrange("p (j c n) -> p j c n", j=PAIRS, c=TOPK)
        taken = [8 * 2 * D]

        def part_of_space(words, dt=F32):
            taken[0] += words
            return space[:, taken[0] - words:taken[0]].bitcast(dt)

        work = space[:, 0:8 * 2 * D].rearrange("p (a b n) -> p a b n", a=4, b=2)
        xT_in = [work[:, 0, s, :].rearrange("p (q k t) -> p q k t", q=2, k=KC) for s in range(2)]
        c_in = [work[:, 1, s, :].rearrange("p (q d) -> p q d", q=2) for s in range(2)]
        cT_in = [work[:, 2, s, :].rearrange("p (q k t) -> p q k t", q=2, k=KC) for s in range(2)]
        turned = work[:, 3, :, :].rearrange("p q (h d) -> p q h d", h=2)
        back = sb("back", [P, 2, 2, D])
        got = part_of_space(2 * KC * T).rearrange("p (q k t) -> p q k t", q=2, k=KC)
        r1 = sb("r1", [P, 2, D])
        st1 = sb("st1", [P, 2, 6])
        mv1 = sb("mv1", [P, 2, 2])
        sd1 = sb("sd1", [P, 2])
        rs1 = sb("rs1", [P, 2])
        x1 = [sb(f"x1_{s}", [P, 2, D]) for s in range(2)]
        x1T = sb("x1T", [P, 2, KC, T])
        att = sb("att", [P, 2, T])
        vabs = sb("vabs", [P, 2])
        vmax = sb("vmax", [P, 2])
        vinv = sb("vinv", [P, 2])
        cs = sb("cs", [P, 2, D])
        r2 = sb("r2", [P, 2, D])
        st2 = sb("st2", [P, 2, 6])
        mv2 = sb("mv2", [P, 2, 2])
        sd2 = sb("sd2", [P, 2])
        rs2 = sb("rs2", [P, 2])
        x2 = [sb(f"x2_{s}", [P, 2, D]) for s in range(2)]
        x2T = sb("x2T", [P, 2, KC, T])
        logits = sb("logits", [P, B, E])
        eps = sb("eps", [P, 1])
        unused = sb("unused", [P, 1])

        w_hi = sb("w_hi", [P, E, W_END], F32R)
        w_lo = sb("w_lo", [P, E, W_END], F32R)
        parts = sb("parts", [P, 4 * RING, KC, P], F32R)
        xT_hi, xT_lo = parts[:, 0:2, :, :], parts[:, 2:4, :, :]
        wv_hi, wv_lo = (parts[:, n:n + 2, :, :].rearrange("p a b c -> p (a b c)").rearrange("p (k d) -> p k d", k=KC)
                        for n in (4, 6))

        shift = [sb(f"shift{s}", [P, 2]) for s in range(2)]
        st_pair, mv_pair, sd_pair, rs_pair = [st1, st2], [mv1, mv2], [sd1, sd2], [rs1, rs2]

        half = sb("half", [P, H_END], F16)
        masked = sb("masked", [P, B, E])
        seen = [logits, masked]
        shifted = sb("shifted", [P, TOPK, B])
        expd = sb("expd", [P, TOPK, B])
        top = sb("top", [P, TOPK, B])
        ties = sb("ties", [P, B, E])
        key = sb("key", [P, B, E])
        kmax = sb("kmax", [P, B])
        pick = sb("pick", [P, TOPK, B, E])
        chosen = sb("chosen", [P, B + 1, E], F16)
        tsum = sb("tsum", [P, B])
        tinv = sb("tinv", [P, B])
        gate = sb("gate", [P, TOPK, B])
        need = sb("need", [P, E])
        upto = [sb(f"upto{n}", [P, 2 * E]) for n in range(4)]
        placed = sb("placed", [P, TOPK, B, E])
        rank = sb("rank", [P, TOPK * B])
        tile_in = sb("tile_in", [P, TOPK * B])
        tile_from = sb("tile_from", [P, TOPK * B])
        part = sb("part", [P, TOPK * B])
        tile_no = sb("tile_no", [P, TOPK * B])
        row_no = sb("row_no", [P, TOPK * B])
        row_neg = sb("row_neg", [P, TOPK * B])
        off = back[:].rearrange("p q h d -> p (q h d)").bitcast(F16)[:, 0:len(ACT_ROWS) * P].rearrange(
            "p (n r) -> p n r", r=P)
        row_hot = part_of_space(TOPK * B * P // 2, F16).rearrange("p (n r) -> p n r", r=P)
        tile_is = part_of_space(TOPK * B * TILES // 2, F16).rearrange("p (n r) -> p n r", r=TILES)
        tile_hot = part_of_space(TOPK * B * TILES // 2, F16).rearrange("p (n r) -> p n r", r=TILES)
        code = sb("code", [P, TILES])
        coded = sb("coded", [P, TILES])
        token = sb("token", [P, TILES])
        second = sb("second", [P, TILES])
        padding = sb("padding", [P, TILES])
        past = angle[:].rearrange("p h d -> p (h d)")[:, 0:TILES * E].rearrange("p (t e) -> p t e", e=E)
        expert = sb("expert", [P, TILES])
        gather_idx = sb("gather_idx", [P, TILES], I32)
        scatter_idx = sb("scatter_idx", [P, TILES], I32)
        gather_now = [sb(f"gather_now{s}", [P, 1], I32) for s in range(RING)]
        scatter_now = [sb(f"scatter_now{s}", [P, 1], I32) for s in range(RING)]
        expert_idx = sb("expert_idx", [P, TILES], I32)

        xs = [turns[:, 0, :], turns[:, 1, :], rem[:, 0, :]]
        xs_hi, xs_lo, hid_hi, hid_lo = ([parts[:, RING * n + s, :, :] for s in range(RING)] for n in range(4))
        silu, hid = cs[:, 0, :], cs[:, 1, :]
        ys = [x1T[:, 0, :, :].rearrange("p k t -> p (k t)"), x1T[:, 1, :, :].rearrange("p k t -> p (k t)"), x2T[:, 0, :, :].rearrange("p k t -> p (k t)")]

        x2_dram = nc.dram_tensor("x2_dram", (N, D), F32, kind="Internal").ap()
        y_dram = nc.dram_tensor("y_dram", (TOPK * N, D), F32, kind="Internal").ap()
        x2_pairs = x2_dram.rearrange("(j q t) d -> j t q d", q=2, t=T)
        y_pairs = y_dram.rearrange("(c j q t) d -> c j t q d", c=TOPK, q=2, t=T)

        p_v = ps("p_v", [P, 2, D])
        p_c = ps("p_c", [P, 2, 2, D])
        p_y = ps("p_y", [P, 2, D])
        p_t = ps("p_t", [P, 2, KC, T])
        p_s = ps("p_s", [P, 2 * D])
        p_a = ps("p_a", [P, 2, D])
        p_r = ps("p_r", [P, 2 * D])
        scores = p_s[:, 0:2 * T].rearrange("p (q s) -> p q s", q=2)
        rowsum = p_r[:, 0:2]
        plog = p_r[:, 64:64 + 2 * E].rearrange("p (q e) -> p q e", q=2)

        p_idle = [p_v[:, 0, 0:P], p_c[:, 0, 0, 0:P]]

        p_place = p_v[:].rearrange("p q d -> p (q d)")[:, 0:(B + 1) * E].rearrange("p (b e) -> p b e", e=E)
        p_inv = p_y[:].rearrange("p q d -> p (q d)")[:, 0:TILES]
        p_up = [p_v[:], p_c[:, 0, :, :], p_c[:, 1, :, :]]
        p_xt = p_y[:].rearrange("p q d -> p (q d)")[:, 0:D].rearrange("p (k t) -> p k t", k=KC)
        p_ht = p_t[:, 0, :, :]
        p_down = [p_s[:, 0:D], p_a[:, 0, :], p_r[:, 0:D]]

        tri = const[:, C_TRI:C_TRI + P]
        ident = const[:, C_IDENT:C_IDENT + P]
        decay = const[:, C_DECAY:C_DECAY + P].rearrange("p (a s) -> p a s", a=1).to_broadcast([P, 2, T])

        const_in, half_in, wv_in, proj_in, freq_in = (sem(n) for n in (
            "const_in", "half_in", "wv_in", "proj_in", "freq_in"))
        carried = sem("carried")
        w_ok = [sem(f"w_ok{s}") for s in range(2)]
        hi_ok, lo_ok = sem("hi_ok"), sem("lo_ok")
        gate_ok, row_no_ok, row_hot2_ok = sem("gate_ok"), sem("row_no_ok"), sem("row_hot2_ok")
        off_ok, row_hot3_ok = sem("off_ok"), sem("row_hot3_ok")
        route, shift_ok, exp_ok, chosen_ok, place_ok = (sem(n) for n in (
            "route", "shift_ok", "exp_ok", "chosen_ok", "place_ok"))
        row_hot_ok, tile_hot_ok, inv_ok, index_ok, x2_saved = (sem(n) for n in (
            "row_hot_ok", "tile_hot_ok", "inv_ok", "index_ok", "x2_saved"))
        xs_ok = [sem(f"xs_ok{s}") for s in range(RING)]
        xt_ok, xhi_ok, xlo_ok, up_ok, silu_ok, hid_ok = (sem(n) for n in (
            "xt_ok", "xhi_ok", "xlo_ok", "up_ok", "silu_ok", "hid_ok"))
        ht_ok, hhi_ok, hlo_ok, down_ok, ys_ok = (sem(n) for n in (
            "ht_ok", "hhi_ok", "hlo_ok", "down_ok", "ys_ok"))
        gather_now_ok, scatter_now_ok = sem("gather_now_ok"), sem("scatter_now_ok")
        put_ok = [sem(f"put_ok{s}") for s in range(RING)]
        x2_back = sem("x2_back")
        y_back = [sem(f"y_back{j}") for j in range(PAIRS)]
        y_in_ok = sem("y_in_ok")
        weighed_ok, sum0_ok, r3_ok, st3_ok, mv3_ok, sd3_ok, rs3_ok, shift3_ok, res_ok = (sem(n) for n in (
            "weighed_ok", "sum0_ok", "r3_ok", "st3_ok", "mv3_ok", "sd3_ok", "rs3_ok", "shift3_ok", "res_ok"))
        out_ok = sem("out_ok")
        x_ok = [sem(f"x_ok{s}") for s in range(2)]
        xT_ok = [sem(f"xT_ok{s}") for s in range(2)]
        c_ok = [sem(f"c_ok{s}") for s in range(2)]
        cT_ok = [sem(f"cT_ok{s}") for s in range(2)]
        zeros_ok, router_in = sem("zeros_ok"), sem("router_in")
        wvhi_ok, wvlo_ok, xThi_ok, xTlo_ok = (sem(n) for n in ("wvhi_ok", "wvlo_ok", "xThi_ok", "xTlo_ok"))
        angle_ok, sine_ok, cosine_ok, rotor_ok = (sem(n) for n in ("angle_ok", "sine_ok", "cosine_ok", "rotor_ok"))
        eps_ok = sem("eps_ok")
        v_ok, turned_ok, sums_ok, back_ok, got_ok, y_ok = (sem(n) for n in (
            "v_ok", "turned_ok", "sums_ok", "back_ok", "got_ok", "y_ok"))
        r1_ok, st1_ok, mv1_ok, sd1_ok, rs1_ok, x1_ok = (sem(n) for n in (
            "r1_ok", "st1_ok", "mv1_ok", "sd1_ok", "rs1_ok", "x1_ok"))
        t1_ok, x1T_ok, sc_ok, att_ok, sum_ok, vabs_ok, vmax_ok, vinv_ok, cs_ok, av_ok = (sem(n) for n in (
            "t1_ok", "x1T_ok", "sc_ok", "att_ok", "sum_ok", "vabs_ok", "vmax_ok", "vinv_ok", "cs_ok", "av_ok"))
        r2_ok, st2_ok, mv2_ok, sd2_ok, rs2_ok, x2_ok = (sem(n) for n in (
            "r2_ok", "st2_ok", "mv2_ok", "sd2_ok", "rs2_ok", "x2_ok"))
        t2_ok, x2T_ok, lg_ok, logits_ok = (sem(n) for n in ("t2_ok", "x2T_ok", "lg_ok", "logits_ok"))
        x2_free = sem("x2_free")
        x2_out = [sem(f"x2_out{s}") for s in range(2)]

        def pipeline(engine, step, first=-1):
            def fixed(i):
                step(i, i % 2, lambda k: 0 <= i + k < PAIRS)
            for i in range(first, 2):
                fixed(i)
            with engine.Fori(1, PAIRS // 2 - 1) as half:
                step(2 * half, 0, lambda k: True)
                step(2 * half + 1, 1, lambda k: True)
            for i in range(PAIRS - 2, PAIRS + 2):
                fixed(i)

        def y_pair(i, c):
            return y_all[:, bass.ds(i, 1), c, :].rearrange("p a (q d) -> p (a q) d", q=2)

        def tile_pipeline(engine, step):
            def fixed(k):
                step(k, lambda d: ((k + d) % RING, (k + d) // RING), lambda d: 0 <= k + d < TILES)
            for k in range(-1, 2 * RING):
                fixed(k)
            last = RING * (TILES // RING - 2)
            with engine.Fori(0, (last - 2 * RING) // UNROLL) as trip:
                for u in range(2 * RING, 2 * RING + UNROLL):
                    step(UNROLL * trip + u, lambda d: ((u + d) % RING, UNROLL // RING * trip + (u + d) // RING),
                         lambda d: True)
            for k in range(last, TILES + 2):
                fixed(k)

        block = scope.enter_context(nc.Block())

        @block.sync
        def _(sp):
            def flat(v):
                names = "abcd"[:len(v.shape) - 1]
                return v.rearrange(f"p {' '.join(names)} -> p ({' '.join(names)})")

            def load(tile, src, ok, j, s):
                sp.dma_start(flat(tile[s]), src[bass.ds(j, 1), :, :].rearrange("a p n -> p (a n)")).then_inc(ok[s], 16)

            def step(i, s, has):
                if has(2):
                    if isinstance(i, int) and i == 0:
                        sp.wait_ge(v_ok, 1)
                    elif has(0):
                        sp.wait_ge(xTlo_ok, i)
                    load(xT_in, xT, xT_ok, i + 2, s)
                if has(1):
                    if has(-1):
                        sp.wait_ge(r1_ok, i)
                    load(x_in, x, x_ok, i + 1, 1 - s)
                    if has(-1):
                        sp.wait_ge(lo_ok, i)
                    load(w_in, weights, w_ok, i + 1, 1 - s)
                if has(-2):
                    sp.wait_ge(x2_ok, i - 1)
                    sp.dma_start(x2_pairs[bass.ds(i - 2, 1), :, :, :].rearrange("a t q d -> t (a q) d"),
                                 x2[s][:]).then_inc(x2_out[s], 16)
                if has(1):
                    if has(-1):
                        sp.wait_ge(sc_ok, i)
                    load(cT_in, ctxT, cT_ok, i + 1, 1 - s)
                    if has(-1):
                        sp.wait_ge(cs_ok, i)
                    load(c_in, ctxt, c_ok, i + 1, 1 - s)
                if has(-2):
                    sp.wait_ge(x2_out[s], 8 * (i - s))
                    sp.sem_inc(x2_free, 1)

            sp.sem_inc(x2_free, 2)
            sp.dma_start(freqs[:], freq).then_inc(freq_in, 16)
            load(xT_in, xT, xT_ok, 0, 0)
            sp.dma_start(wv[:], wvT).then_inc(wv_in, 16)
            sp.dma_start(const[:], consts).then_inc(const_in, 16)
            sp.dma_start(wo[:], woT).then_inc(proj_in, 16)
            step(-1, 1, lambda k: k in (1, 2))
            sp.dma_start(wr[:], routerT).then_inc(router_in, 16)
            sp.dma_start(half[:], halves).then_inc(half_in, 16)
            pipeline(sp, step, 0)
            sp.sem_inc(x2_saved, 1)
            sp.dma_start(x2_keep.rearrange("p j n -> p (j n)").rearrange("p (j q d) -> p (j q) d", q=2, d=D),
                         x2_dram.rearrange("(j t) d -> t j d", t=T)).then_inc(x2_back, 16)

            for s in range(RING):
                sp.wait_ge(put_ok[s], 16 * (TILES // RING))

            def load_rows(j):
                for c in range(TOPK):
                    sp.dma_start(y_all[:, j, c, :].rearrange("p (q d) -> p q d", q=2), y_pairs[c, j]).then_inc(
                        y_back[j], 16)

            for j in range(AHEAD):
                load_rows(j)
            for j in range(PAIRS):
                sp.wait_ge(y_back[j], 32)
                sp.sem_inc(y_in_ok, 1)
                if j + AHEAD < PAIRS:
                    load_rows(j + AHEAD)
            for j in range(PAIRS):
                sp.wait_ge(res_ok, j + 1)
                sp.dma_start(out[j], y_all[:, j, 1, :]).then_inc(out_ok, 16)
            sp.wait_ge(out_ok, 16 * PAIRS)

        @block.tensor
        def _(pe):
            def keep_busy(matmuls, data, bank):
                for _ in range(matmuls):
                    nc.tensor.matmul(p_idle[bank], data, data, start=True, stop=True)

            pe.wait_ge(zeros_ok, 1)
            keep_busy(10, key[:].rearrange("p b e -> p (b e)"), 1)
            pe.wait_ge(wv_in, 16)

            def values(q, first):
                terms = ((xT_in[0], wv),) if first else ((xT_hi, wv_hi), (xT_hi, wv_lo), (xT_lo, wv_hi))
                for n, (xT_part, wv_part) in enumerate(terms):
                    for k in range(KC):
                        last = nc.tensor.matmul(p_v[:, q, :], xT_part[:, q, k, :], wv_part[:, k, :],
                                                start=(n == k == 0), stop=(n == len(terms) - 1 and k == KC - 1))
                return last

            def step(i, s, has):
                if isinstance(i, int) and i == 0:
                    pe.wait_ge(const_in, 16)
                    pe.wait_ge(proj_in, 16)
                    pe.wait_ge(wvlo_ok, 1)
                if isinstance(i, int) and i == 1:
                    pe.wait_ge(router_in, 16)
                idle = FILL[i - PAIRS + 1] if isinstance(i, int) and i >= PAIRS - 1 else (0, 0, 0, 0, 0)
                if has(0):
                    pe.wait_ge(turned_ok, i + 1)
                    for q in range(2):
                        for h in range(2):
                            for k in range(KC):
                                last = nc.tensor.matmul(p_c[:, q, h, k * T:(k + 1) * T],
                                                        turned[:, q, h, k * P:(k + 1) * P], tri,
                                                        start=True, stop=True)
                    last.then_inc(sums_ok, 1)
                if has(-1):
                    keep_busy(idle[0], ident, 0)
                    pe.wait_ge(x1_ok, i)
                    for q in range(2):
                        for k in range(KC):
                            last = nc.tensor.transpose(p_t[:, q, k, :], x1[1 - s][:, q, k * P:(k + 1) * P], ident)
                    last.then_inc(t1_ok, 1)
                if has(1):
                    first = not has(0)
                    if first:
                        pe.wait_ge(xT_ok[0], 16)
                    else:
                        pe.wait_ge(xTlo_ok, i + 1)
                        pe.wait_ge(turned_ok, i + 1)
                    values(0, first)
                if has(-1):
                    keep_busy(idle[1], ident, 0)
                    pe.wait_ge(cT_ok[1 - s], 8 * (i - 1 - (1 - s)) + 16)
                    pe.wait_ge(x1T_ok, i)
                    if has(-2):
                        pe.wait_ge(att_ok, i - 1)
                    for q in range(2):
                        for k in range(KC):
                            last = nc.tensor.matmul(scores[:, q, :], cT_in[1 - s][:, q, k, :], x1T[:, q, k, :],
                                                    start=(k == 0), stop=(k == KC - 1))
                    last.then_inc(sc_ok, 1)
                if has(1):
                    values(1, first).then_inc(v_ok, 1)
                if has(-1):
                    keep_busy(idle[2], ident, 0)
                    pe.wait_ge(att_ok, i)
                    for q in range(2):
                        last = nc.tensor.matmul(rowsum[:, q:q + 1], att[:, q, :], const[:, C_ONE:C_ONE + 1],
                                                start=True, stop=True)
                    last.then_inc(sum_ok, 1)
                if has(0):
                    pe.wait_ge(got_ok, i + 1)
                    for q in range(2):
                        for k in range(KC):
                            last = nc.tensor.matmul(p_y[:, q, :], got[:, q, k, :], wo[:, k, :],
                                                    start=(k == 0), stop=(k == KC - 1))
                    last.then_inc(y_ok, 1)
                if has(-2):
                    if not has(-1):
                        keep_busy(idle[0], ident, 0)
                    pe.wait_ge(x2_ok, i - 1)
                    if has(-1):
                        pe.wait_ge(x1T_ok, i)
                    for q in range(2):
                        for k in range(KC):
                            last = nc.tensor.transpose(p_t[:, q, k, :], x2[s][:, q, k * P:(k + 1) * P], ident)
                    last.then_inc(t2_ok, 1)
                if has(-1):
                    keep_busy(idle[3], ident, 0)
                    pe.wait_ge(cs_ok, i)
                    if has(-2):
                        pe.wait_ge(r2_ok, i - 1)
                    for q in range(2):
                        last = nc.tensor.matmul(p_a[:, q, :], att[:, q, :], cs[:, q, :], start=True, stop=True)
                    last.then_inc(av_ok, 1)
                if has(-2):
                    keep_busy(idle[4], ident, 0)
                    pe.wait_ge(x2T_ok, i - 1)
                    if has(-1):
                        pe.wait_ge(vabs_ok, i)
                    for q in range(2):
                        for k in range(KC):
                            last = nc.tensor.matmul(plog[:, q, :], x2T[:, q, k, :], wr[:, k, :],
                                                    start=(k == 0), stop=(k == KC - 1))
                    last.then_inc(lg_ok, 1)

            pipeline(pe, step)

            pe.wait_ge(half_in, 16)
            def before(first, end, new):
                return nc.tensor.matmul(p_place[:, first:end, :], half[:, H_STRICT:H_STRICT + P], chosen[:, first:end, :],
                                        start=new, stop=True, skip_group_check=True)

            def above(b, new):
                return nc.tensor.matmul(p_place[:, b + 1:, :], half[:, H_ONES:H_ONES + P],
                                        chosen[:, b:b + 1, :].to_broadcast([P, B - b, E]),
                                        start=new, stop=True, skip_group_check=True)

            pe.wait_ge(chosen_ok, 2)
            before(0, 1, True)
            above(0, True)
            before(1, B - LATE, False)
            for b in range(1, B - LATE):
                above(b, False)
            keep_busy(5, ident, 1)
            pe.wait_ge(chosen_ok, 3)
            before(B - LATE, B, False)
            for b in range(B - LATE, B):
                last = above(b, False)
            last.then_inc(place_ok, 1)
            keep_busy(20, ident, 1)
            pe.wait_ge(tile_hot_ok, 1)
            for rows, ok in ((POOL_ROWS, row_hot2_ok), (DVE_ROWS, row_hot_ok), (ACT_ROWS, row_hot3_ok)):
                for n in rows:
                    pe.wait_ge(ok, n - rows[0] + 1 if ok is not row_hot3_ok else 1)
                    last = nc.tensor.matmul(p_inv, row_hot[:, n, :], tile_hot[:, n, :],
                                            start=(n == POOL_ROWS[0]), stop=(n == ACT_ROWS[-1]))
            last.then_inc(inv_ok, 1)
            keep_busy(12, ident, 1)
            pe.wait_ge(index_ok, 1)

            def split_product(dst, lhs_hi, lhs_lo, col, width, start):
                n = 0
                for lhs, w in ((lhs_hi, w_hi), (lhs_hi, w_lo), (lhs_lo, w_hi)):
                    for k in range(KC):
                        last = nc.tensor.matmul(dst, lhs[:, k, :],
                                                w[:].rearrange("p e n -> p (e n)")[:, bass.ds(start + col + k * width, width)],
                                                start=(n == 0), stop=(n == 3 * KC - 1))
                        n += 1
                return last

            count = [0]

            def weights_at(k, name):
                count[0] += 1
                register = pe.alloc_register(f"{name}{count[0]}")
                pe.reg_load(register, expert_idx[0:1, bass.ds(k, 1)])
                return pe.snap(register, donate=True, min_val=0, max_val=(E - 1) * W_END)

            def tile(k, at, has):
                if has(-2):
                    down_at = weights_at(k - 2, "down_at")
                if has(0):
                    up_at = weights_at(k, "up_at")
                if has(1):
                    s, used = at(1)
                    pe.wait_ge(xs_ok[s], 16 * used + 16)
                    if has(0):
                        pe.wait_ge(xlo_ok, k + 1)
                    for c in range(KC):
                        last = nc.tensor.transpose(p_xt[:, c, :], xs[s][:, c * P:(c + 1) * P], ident)
                    last.then_inc(xt_ok, 1)
                if has(0):
                    s, _ = at(0)
                    pe.wait_ge(xlo_ok, k + 1)
                    if has(-3):
                        pe.wait_ge(hid_ok, k - 2)
                    split_product(p_up[s], xs_hi[s], xs_lo[s], W_UP, 2 * DH, up_at).then_inc(up_ok, 1)
                if has(-1):
                    pe.wait_ge(hid_ok, k)
                    if has(-2):
                        pe.wait_ge(hlo_ok, k - 1)
                    for c in range(KC):
                        last = nc.tensor.transpose(p_ht[:, c, :], hid[:, c * P:(c + 1) * P], ident)
                    last.then_inc(ht_ok, 1)
                if has(-2):
                    s, _ = at(-2)
                    pe.wait_ge(hlo_ok, k - 1)
                    if has(-5):
                        pe.wait_ge(ys_ok, k - 4)
                    split_product(p_down[s], hid_hi[s], hid_lo[s], W_DOWN, D, down_at).then_inc(down_ok, 1)

            tile_pipeline(pe, tile)

        @block.vector
        def _(dve):
            dve.wait_ge(freq_in, 16)
            nc.vector.memset(eps[:], EPS).then_inc(eps_ok, 1)
            count = [0]

            def after(ins):
                count[0] += 1
                ins.then_inc(angle_ok, 1)
                dve.wait_ge(angle_ok, count[0])

            def angles(h):
                a, t, r = angle[:, h, :], turns[:, h, :], rem[:, h, :]
                if h == 0:
                    after(nc.vector.tensor_scalar(a, frow, tok, None, ALU.mult))
                else:
                    for k in range(KC):
                        after(nc.vector.tensor_scalar(angle[:, 1, k * T:(k + 1) * T], const[:, C_ROW:C_ROW + P],
                                                      fcol[:, k:k + 1], None, ALU.mult))
                after(nc.vector.tensor_scalar(t, a, 1.0 / TWO_PI, ROUND, ALU.mult, ALU.add))
                after(nc.vector.tensor_scalar(r, t, -ROUND, None, ALU.add))
                after(nc.vector.scalar_tensor_tensor(t, r, -TURN_HI, a, ALU.mult, ALU.add))

            def arguments(h):
                a, t, r = angle[:, h, :], turns[:, h, :], rem[:, h, :]
                after(nc.vector.scalar_tensor_tensor(a, r, -TURN_MID, t, ALU.mult, ALU.add))
                after(nc.vector.scalar_tensor_tensor(t, r, -TURN_LO, a, ALU.mult, ALU.add))
                nc.vector.tensor_scalar(a, t, SIN_MAX, -SIN_MAX, ALU.min, ALU.max).then_inc(sine_ok, 1)
                dve.wait_ge(sine_ok, h + 1)
                after(nc.vector.scalar_tensor_tensor(t, a, -1.0, a, ALU.mult, ALU.min))
                nc.vector.tensor_scalar(r, t, np.pi / 2, None, ALU.add).then_inc(cosine_ok, 1)

            angles(0)
            arguments(0)
            dve.wait_ge(const_in, 16)
            angles(1)

            def statistics(j, src, st, mv, r_ok, st_ok, mv_ok):
                dve.wait_ge(r_ok, j + 1)
                for q in range(2):
                    nc.vector.bn_stats(st[:, q, :], src[:, q, :]).then_inc(st_ok, 1)
                dve.wait_ge(st_ok, 2 * j + 2)
                dve.sem_inc(carried, 1)
                for q in range(2):
                    nc.vector.bn_aggr(mv[:, q, :], st[:, q, :]).then_inc(mv_ok, 1)

            def normalise(j, src, mv, sd, rs, dst, sd_ok, rs_ok, dst_ok):
                dve.wait_ge(sd_ok, j + 1)
                nc.vector.reciprocal(rs[:], sd[:]).then_inc(rs_ok, 1)
                dve.wait_ge(rs_ok, j + 1)
                for q in range(2):
                    last = nc.vector.tensor_scalar(dst[:, q, :], src[:, q, :], mv[:, q, 0:1], rs[:, q:q + 1],
                                                   ALU.subtract, ALU.mult)
                last.then_inc(dst_ok, 1)

            def turn(j):
                dve.wait_ge(v_ok, j + 1)
                for q in range(2):
                    last = nc.vector.tensor_tensor(
                        turned[:, q, :, :], p_v[:, q:q + 1, :].to_broadcast([P, 2, D]), rotor[:, 0, :, :], ALU.mult)
                last.then_inc(turned_ok, 1)

            links = [0]

            def link(ins):
                links[0] += 1
                ins.then_inc(route, 1)
                dve.wait_ge(route, links[0])

            def select(first, end):
                b = slice(first, end)

                def over_e(v):
                    return v.unsqueeze(2).to_broadcast([P, end - first, E])

                pref = const[:, C_PREF:C_PREF + E].unsqueeze(1).to_broadcast([P, end - first, E])
                dve.wait_ge(logits_ok, end // 2)
                for c in range(TOPK):
                    link(nc.vector.tensor_reduce(top[:, c, b], seen[c][:, b, :], AX_X, ALU.max))
                    link(nc.vector.tensor_tensor(ties[:, b, :], seen[c][:, b, :], over_e(top[:, c, b]), ALU.is_equal))
                    link(nc.vector.tensor_tensor(key[:, b, :], ties[:, b, :], pref, ALU.mult))
                    link(nc.vector.tensor_reduce(kmax[:, b], key[:, b, :], AX_X, ALU.max))
                    link(nc.vector.tensor_tensor(pick[:, c, b, :], key[:, b, :], over_e(kmax[:, b]), ALU.is_equal))
                    if c == 0:
                        link(nc.vector.scalar_tensor_tensor(masked[:, b, :], pick[:, 0, b, :], -MASKED, logits[:, b, :],
                                                            ALU.mult, ALU.add))
                nc.vector.tensor_tensor(chosen[:, b, :], pick[:, 0, b, :], pick[:, 1, b, :], ALU.add).then_inc(chosen_ok, 1)

            def step(i, s, has):
                if has(-2):
                    dve.wait_ge(av_ok, i - 1)
                    nc.vector.tensor_tensor(r2[:], p_a[:], x1[s][:], ALU.add).then_inc(r2_ok, 1)
                if has(-1):
                    normalise(i - 1, r1, mv1, sd1, rs1, x1[1 - s], sd1_ok, rs1_ok, x1_ok)
                if has(0):
                    dve.wait_ge(sums_ok, i + 1)
                    if isinstance(i, int) and i == 0:
                        dve.wait_ge(rotor_ok, 4)
                    if has(-1):
                        dve.wait_ge(got_ok, i)
                    for q in range(2):
                        last = nc.vector.tensor_tensor(back[:, q, :, :], p_c[:, q, :, :], rotor[:, 1, :, :], ALU.mult)
                    last.then_inc(back_ok, 1)
                if has(-2):
                    statistics(i - 2, r2, st2, mv2, r2_ok, st2_ok, mv2_ok)
                if has(-1):
                    dve.wait_ge(sc_ok, i)
                    nc.vector.tensor_tensor(att[:], scores, decay, ALU.mult).then_inc(att_ok, 1)
                if has(-2):
                    dve.wait_ge(x2_free, i - 1)
                    normalise(i - 2, r2, mv2, sd2, rs2, x2[s], sd2_ok, rs2_ok, x2_ok)
                if has(-1):
                    dve.wait_ge(vabs_ok, i)
                    nc.vector.tensor_scalar(vmax[:], vabs[:], 1.0, None, ALU.max).then_inc(vmax_ok, 1)
                    dve.wait_ge(vmax_ok, i)
                    nc.vector.reciprocal(vinv[:], vmax[:]).then_inc(vinv_ok, 1)
                if isinstance(i, int) and i == PAIRS:
                    nc.vector.memset(chosen[:, B, :], 0.0).then_inc(chosen_ok, 1)
                    for n in range(4):
                        link(nc.vector.memset(upto[n][:], 0.0))
                    select(0, B - LATE)
                if has(1):
                    if isinstance(i, int) and i == -1:
                        dve.wait_ge(rotor_ok, 2)
                    turn(i + 1)
                    if isinstance(i, int) and i == -1:
                        arguments(1)
                if has(0):
                    dve.wait_ge(y_ok, i + 1)
                    dve.wait_ge(x_ok[s], 8 * (i - s) + 16)
                    nc.vector.tensor_tensor(r1[:], p_y[:], x_in[s], ALU.add).then_inc(r1_ok, 1)
                    statistics(i, r1, st1, mv1, r1_ok, st1_ok, mv1_ok)

            pipeline(dve, step)

            select(B - LATE, B)
            nc.vector.tensor_tensor(shifted[:], top[:], top[:, 0:1, :].to_broadcast([P, TOPK, B]), ALU.subtract).then_inc(shift_ok, 1)
            dve.wait_ge(place_ok, 1)
            def both(a, b):
                links[0] += 2
                a.then_inc(route, 1)
                b.then_inc(route, 1)
                dve.wait_ge(route, links[0])

            both(nc.vector.tensor_tensor(placed[:], pick[:], p_place[:, 0:B, :].unsqueeze(1).to_broadcast([P, TOPK, B, E]),
                                         ALU.mult),
                 nc.vector.tensor_scalar(need[:], p_place[:, B, :], HALF, 1.0 / P, ALU.add, ALU.mult))
            both(nc.vector.tensor_reduce(rank[:], placed[:].rearrange("p c b e -> p (c b) e"), AX_X, ALU.add),
                 nc.vector.tensor_scalar(upto[0][:, E:], need[:], ROUND, -ROUND, ALU.add, ALU.add))

            def running(n):
                by = 2 ** n
                return nc.vector.tensor_tensor(upto[n + 1][:, E:], upto[n][:, E:], upto[n][:, E - by:2 * E - by], ALU.add)

            both(nc.vector.tensor_scalar(part[:], rank[:], -HALF, 1.0 / P, ALU.add, ALU.mult), running(0))
            both(nc.vector.tensor_scalar(tile_in[:], part[:], ROUND, -ROUND, ALU.add, ALU.add), running(1))
            nc.vector.scalar_tensor_tensor(row_no[:], tile_in[:], -float(P), rank[:], ALU.mult, ALU.add).then_inc(row_no_ok, 1)
            nc.vector.scalar_tensor_tensor(row_neg[:], tile_in[:], float(P), rank[:], ALU.mult, ALU.subtract).then_inc(row_no_ok, 1)
            link(running(2))
            base = upto[3][:, E - 1:2 * E - 1].unsqueeze(1).unsqueeze(1).to_broadcast([P, TOPK, B, E])
            link(nc.vector.tensor_tensor(placed[:], pick[:], base, ALU.mult))
            link(nc.vector.tensor_reduce(tile_from[:], placed[:].rearrange("p c b e -> p (c b) e"), AX_X, ALU.add))
            link(nc.vector.tensor_tensor(tile_no[:], tile_from[:], tile_in[:], ALU.add))
            tiles_row = half[:, H_ROW:H_ROW + TILES].unsqueeze(1).to_broadcast([P, TOPK * B, TILES])
            link(nc.vector.tensor_tensor(tile_is, tiles_row, tile_no[:].unsqueeze(2).to_broadcast([P, TOPK * B, TILES]),
                                         ALU.is_equal))
            codes = half[:, H_CODE:H_CODE + TOPK * B].unsqueeze(2).to_broadcast([P, TOPK * B, TILES])
            nc.vector.tensor_tensor(tile_hot, tile_is, codes, ALU.mult).then_inc(tile_hot_ok, 1)
            dve.wait_ge(row_no_ok, 1)
            for n in DVE_ROWS:
                nc.vector.tensor_scalar(row_hot[:, n, :], half[:, H_ROW:H_ROW + P], row_no[:, n:n + 1], None,
                                        ALU.is_equal).then_inc(row_hot_ok, 1)
            dve.wait_ge(inv_ok, 1)
            link(nc.vector.tensor_copy(code[:], p_inv))
            link(nc.vector.scalar_tensor_tensor(coded[:], code[:], -1.0, code[:], ALU.mult, ALU.max))
            link(nc.vector.tensor_scalar(gather_idx[:], coded[:], -1.0, 0.0, ALU.add, ALU.max))
            for k in range(RING):
                nc.vector.tensor_copy(gather_now[k][:], gather_idx[:, k:k + 1]).then_inc(gather_now_ok, 1)
            link(nc.vector.tensor_tensor(past, const[:, C_ROW:C_ROW + TILES].unsqueeze(2).to_broadcast([P, TILES, E]),
                                         upto[3][:, E:].unsqueeze(1).to_broadcast([P, TILES, E]), ALU.is_ge))
            link(nc.vector.tensor_reduce(expert[:], past, AX_X, ALU.add))
            nc.vector.tensor_scalar(expert_idx[:], expert[:], float(E - 1), float(W_END), ALU.min, ALU.mult).then_inc(index_ok, 1)
            nc.vector.tensor_scalar(token[:], coded[:], -1.0, 0.0, ALU.add, ALU.max).then_inc(index_ok, 1)
            nc.vector.tensor_scalar(second[:], code[:], 0.0, float(N), ALU.is_lt, ALU.mult).then_inc(index_ok, 1)
            nc.vector.tensor_scalar(padding[:], code[:], 0.0, float(SKIP), ALU.is_equal, ALU.mult).then_inc(index_ok, 1)
            dve.wait_ge(index_ok, 4)
            link(nc.vector.tensor_tensor(coded[:], token[:], second[:], ALU.add))
            link(nc.vector.tensor_tensor(scatter_idx[:], coded[:], padding[:], ALU.add))
            dve.wait_ge(exp_ok, 1)
            link(nc.vector.tensor_tensor(tsum[:], expd[:, 0, :], expd[:, 1, :], ALU.add))
            link(nc.vector.reciprocal(tinv[:], tsum[:]))
            nc.vector.tensor_tensor(gate[:], expd[:], tinv[:].unsqueeze(1).to_broadcast([P, TOPK, B]), ALU.mult).then_inc(gate_ok, 1)

            def tile(k, at, has):
                if has(1):
                    s, _ = at(1)
                    dve.wait_ge(xhi_ok, k + 2)
                    nc.vector.tensor_tensor(xs_lo[s], p_xt, xs_hi[s].bitcast(F32), ALU.subtract).then_inc(xlo_ok, 1)
                if has(4):
                    s, _ = at(1)
                    nc.vector.tensor_copy(gather_now[s][:], gather_idx[:, bass.ds(k + 4, 1)]).then_inc(gather_now_ok, 1)
                if has(0):
                    s, _ = at(0)
                    dve.wait_ge(silu_ok, k + 1)
                    if has(-1):
                        dve.wait_ge(ht_ok, k)
                    up_rows = p_up[s].rearrange("p q d -> p (q d)")[:, DH:2 * DH]
                    nc.vector.tensor_tensor(hid, up_rows, silu, ALU.mult).then_inc(hid_ok, 1)
                if has(-1):
                    s, _ = at(-1)
                    dve.wait_ge(hhi_ok, k)
                    nc.vector.tensor_tensor(hid_lo[s], p_ht, hid_hi[s].bitcast(F32), ALU.subtract).then_inc(hlo_ok, 1)
                if has(-2):
                    s, _ = at(-2)
                    if has(-5):
                        dve.wait_ge(put_ok[s], 16 * at(-2)[1])
                    nc.vector.tensor_copy(scatter_now[s][:], scatter_idx[:, bass.ds(k - 2, 1)]).then_inc(scatter_now_ok, 1)

            tile_pipeline(dve, tile)

            def finish(i, s, has):
                if has(0):
                    dve.wait_ge(sum0_ok, i + 1)
                    for q in range(2):
                        last = nc.vector.scalar_tensor_tensor(
                            y_pair(i, 0)[:, q, :], y_pair(i, 1)[:, q, :], gate[:, 1, bass.ds(2 * i + q, 1)],
                            y_pair(i, 0)[:, q, :], ALU.mult, ALU.add)
                    last.then_inc(r3_ok, 1)
                if has(-1):
                    dve.wait_ge(sd3_ok, i)
                    nc.vector.reciprocal(rs_pair[1 - s][:], sd_pair[1 - s][:]).then_inc(rs3_ok, 1)
                if has(0):
                    dve.wait_ge(r3_ok, i + 1)
                    dve.sem_inc(carried, 1)
                    for q in range(2):
                        nc.vector.bn_stats(st_pair[s][:, q, :], y_pair(i, 0)[:, q, :]).then_inc(st3_ok, 1)
                if has(-1):
                    dve.wait_ge(rs3_ok, i)
                    nc.vector.scalar_tensor_tensor(shift[1 - s][:], mv_pair[1 - s][:, :, 0], -1.0, rs_pair[1 - s][:],
                                                   ALU.mult, ALU.mult).then_inc(shift3_ok, 1)
                if has(0):
                    dve.wait_ge(st3_ok, 2 * i + 2)
                    dve.sem_inc(carried, 1)
                    for q in range(2):
                        nc.vector.bn_aggr(mv_pair[s][:, q, :], st_pair[s][:, q, :]).then_inc(mv3_ok, 1)

            pipeline(dve, finish, 0)

        @block.scalar
        def _(act):
            act.wait_ge(wv_in, 16)
            nc.scalar.activation(wv_hi, wv[:], ACT.Copy).then_inc(wvhi_ok, 1)
            for h in range(2):
                if h == 1:
                    act.wait_ge(xT_ok[1], 16)
                    nc.scalar.activation(xT_hi, xT_in[1], ACT.Copy).then_inc(xThi_ok, 1)
                act.wait_ge(sine_ok, h + 1)
                nc.scalar.activation(rotor[:, h, 1, :], angle[:, h, :], ACT.Sin).then_inc(rotor_ok, 1)
                act.wait_ge(cosine_ok, h + 1)
                nc.scalar.activation(rotor[:, h, 0, :], rem[:, h, :], ACT.Sin).then_inc(rotor_ok, 1)
            act.wait_ge(eps_ok, 1)

            def step(i, s, has):
                if has(-1):
                    act.wait_ge(mv1_ok, 2 * i)
                    nc.scalar.activation(sd1[:], mv1[:, :, 1], ACT.Sqrt, bias=eps[:]).then_inc(sd1_ok, 1)
                    act.wait_ge(t1_ok, i)
                    nc.scalar.activation(x1T[:], p_t[:], ACT.Copy).then_inc(x1T_ok, 1)
                if has(-2):
                    act.wait_ge(mv2_ok, 2 * i - 2)
                    nc.scalar.activation(sd2[:], mv2[:, :, 1], ACT.Sqrt, bias=eps[:]).then_inc(sd2_ok, 1)
                if has(-1):
                    act.wait_ge(sum_ok, i)
                    nc.scalar.activation(vabs[:], rowsum, ACT.Abs).then_inc(vabs_ok, 1)
                if has(2) and has(0):
                    act.wait_ge(xT_ok[s], 8 * (i - s) + 32)
                    act.wait_ge(v_ok, i + 2)
                    nc.scalar.activation(xT_hi, xT_in[s], ACT.Copy).then_inc(xThi_ok, 1)
                if has(0):
                    act.wait_ge(w_ok[s], 8 * (i - s) + 16)
                    nc.scalar.activation(w_hi[:, bass.ds(i, 1), :].rearrange("p a n -> p (a n)"), w_in[s],
                                         ACT.Copy).then_inc(hi_ok, 1)
                if has(-2):
                    act.wait_ge(t2_ok, i - 1)
                    nc.scalar.activation(x2T[:], p_t[:], ACT.Copy).then_inc(x2T_ok, 1)
                    act.wait_ge(lg_ok, i - 1)
                    nc.scalar.activation(logits[:, bass.ds(2 * (i - 2), 2), :], plog, ACT.Copy).then_inc(logits_ok, 1)

            pipeline(act, step)

            act.wait_ge(shift_ok, 1)
            nc.scalar.activation(expd[:], shifted[:], ACT.Exp).then_inc(exp_ok, 1)
            act.wait_ge(half_in, 16)
            act.wait_ge(row_no_ok, 2)
            for n in ACT_ROWS:
                nc.scalar.activation(off[:, n - ACT_ROWS[0], :], half[:, H_ROW:H_ROW + P], ACT.Abs,
                                     bias=row_neg[:, n:n + 1]).then_inc(off_ok, 1)
            act.wait_ge(off_ok, len(ACT_ROWS))
            nc.scalar.activation(row_hot[:, ACT_ROWS[0]:, :], off, ACT.Relu, bias=const[:, C_ONE:C_ONE + 1],
                                 scale=-1.0).then_inc(row_hot3_ok, 1)
            nc.scalar.activation(unused[:], eps[:], ACT.Silu)

            def tile(k, at, has):
                if has(1):
                    s, _ = at(1)
                    act.wait_ge(xt_ok, k + 2)
                    nc.scalar.activation(xs_hi[s], p_xt, ACT.Copy).then_inc(xhi_ok, 1)
                if has(0):
                    s, _ = at(0)
                    act.wait_ge(up_ok, k + 1)
                    if has(-1):
                        act.wait_ge(hid_ok, k)
                    gate_rows = p_up[s].rearrange("p q d -> p (q d)")[:, 0:DH]
                    nc.scalar.activation(silu, gate_rows, ACT.Silu).then_inc(silu_ok, 1)
                if has(-1):
                    s, _ = at(-1)
                    act.wait_ge(ht_ok, k)
                    if has(-4):
                        act.wait_ge(down_ok, k - 3)
                    nc.scalar.activation(hid_hi[s], p_ht, ACT.Copy).then_inc(hhi_ok, 1)
                if has(-2):
                    s, used = at(-2)
                    act.wait_ge(down_ok, k - 1)
                    if has(-5):
                        act.wait_ge(put_ok[s], 16 * used)
                    nc.scalar.activation(ys[s], p_down[s], ACT.Copy).then_inc(ys_ok, 1)

            tile_pipeline(act, tile)

            act.wait_ge(gate_ok, 1)
            nc.scalar.activation(unused[:], eps[:], ACT.Sqrt)

            def weigh(j):
                act.wait_ge(y_in_ok, j + 1)
                for q in range(2):
                    nc.scalar.activation(y_pair(j, 0)[:, q, :], y_pair(j, 0)[:, q, :], ACT.Copy,
                                         scale=gate[:, 0, bass.ds(2 * j + q, 1)]).then_inc(weighed_ok, 1)

            def finish(i, s, has):
                if isinstance(i, int) and i == -1:
                    weigh(0)
                if has(2):
                    weigh(i + 2)
                if has(0):
                    act.wait_ge(mv3_ok, 2 * i + 2)
                    nc.scalar.activation(sd_pair[s][:], mv_pair[s][:, :, 1], ACT.Sqrt, bias=eps[:]).then_inc(sd3_ok, 1)
                if has(-1):
                    act.wait_ge(shift3_ok, i)
                    for q in range(2):
                        last = nc.scalar.activation(y_pair(i - 1, 1)[:, q, :], y_pair(i - 1, 0)[:, q, :], ACT.Identity,
                                                    scale=rs_pair[1 - s][:, q:q + 1], bias=shift[1 - s][:, q:q + 1])
                    last.then_inc(res_ok, 1)

            pipeline(act, finish)

        @block.gpsimd
        def _(pool):
            nc.gpsimd.memset(key[:], 0.0).then_inc(zeros_ok, 1)
            pool.wait_ge(wvhi_ok, 1)
            nc.gpsimd.tensor_tensor(wv_lo, wv[:], wv_hi.bitcast(F32), ALU.subtract).then_inc(wvlo_ok, 1)

            def step(i, s, has):
                if has(0):
                    pool.wait_ge(back_ok, i + 1)
                    if has(-1):
                        pool.wait_ge(y_ok, i)
                    nc.gpsimd.tensor_tensor(got, back[:, :, 0, :].rearrange("p q (k t) -> p q k t", k=KC),
                                            back[:, :, 1, :].rearrange("p q (k t) -> p q k t", k=KC), ALU.add).then_inc(got_ok, 1)
                if has(-1):
                    pool.wait_ge(c_ok[1 - s], 8 * (i - 1 - (1 - s)) + 16)
                    pool.wait_ge(vinv_ok, i)
                    if has(-2):
                        pool.wait_ge(av_ok, i - 1)
                    for q in range(2):
                        last = nc.gpsimd.tensor_tensor(cs[:, q, :], c_in[1 - s][:, q, :], vinv[:, q:q + 1].to_broadcast([P, D]), ALU.mult)
                    last.then_inc(cs_ok, 1)

                if has(2):
                    pool.wait_ge(xThi_ok, i + 2)
                    nc.gpsimd.tensor_tensor(xT_lo, xT_in[s], xT_hi.bitcast(F32), ALU.subtract).then_inc(xTlo_ok, 1)
                if has(0):
                    pool.wait_ge(hi_ok, i + 1)
                    nc.gpsimd.tensor_tensor(w_lo[:, bass.ds(i, 1), :].rearrange("p a n -> p (a n)"), w_in[s],
                                            w_hi[:, bass.ds(i, 1), :].rearrange("p a n -> p (a n)").bitcast(F32),
                                            ALU.subtract).then_inc(lo_ok, 1)

            pipeline(pool, step)

            pool.wait_ge(half_in, 16)
            pool.wait_ge(row_no_ok, 1)
            for n in POOL_ROWS:
                nc.gpsimd.tensor_scalar(row_hot[:, n, :], half[:, H_ROW:H_ROW + P], row_no[:, n:n + 1], None,
                                        ALU.is_equal).then_inc(row_hot2_ok, 1)

            def gather(s):
                nc.gpsimd.indirect_dma_start(xs[s], None, x2_dram,
                                             bass.IndirectOffsetOnAxis(ap=gather_now[s][:], axis=0)).then_inc(xs_ok[s], 16)

            pool.wait_ge(x2_saved, 1)
            for k in range(RING):
                pool.wait_ge(gather_now_ok, k + 1)
                gather(k)

            def tile(k, at, has):
                if has(4):
                    s, _ = at(1)
                    pool.wait_ge(gather_now_ok, k + 5)
                    pool.sem_inc(carried, 1)
                    gather(s)
                if has(-2):
                    s, _ = at(-2)
                    pool.wait_ge(scatter_now_ok, k - 1)
                    pool.wait_ge(ys_ok, k - 1)
                    pool.sem_inc(carried, 1)
                    nc.gpsimd.indirect_dma_start(
                        y_dram, bass.IndirectOffsetOnAxis(ap=scatter_now[s][:], axis=0),
                        ys[s], None, bounds_check=TOPK * N - 1, oob_is_err=False).then_inc(put_ok[s], 16)

            tile_pipeline(pool, tile)

            pool.wait_ge(x2_back, 16)

            def finish(i, s, has):
                if has(1):
                    pool.wait_ge(weighed_ok, 2 * i + 4)
                    nc.gpsimd.tensor_tensor(y_pair(i + 1, 0), y_pair(i + 1, 0),
                                            x2_keep[:, bass.ds(i + 1, 1), :].rearrange("p a (q d) -> p (a q) d", q=2),
                                            ALU.add).then_inc(sum0_ok, 1)

            pipeline(pool, finish)


def kernel(**inputs):
    import numpy as _np
    import concourse.bacc as _bacc
    from concourse import mybir as _mybir
    from concourse.bass_utils import run_bass_kernel_spmd as _run

    a = {k: _np.asarray(v) for k, v in inputs.items()}

    def rows(v):
        return v.reshape(PAIRS, 2, T, D).transpose(0, 2, 1, 3).reshape(PAIRS, P, 2 * D)

    def columns(v):
        return v.reshape(PAIRS, 2, T, KC, P).transpose(0, 4, 1, 3, 2).reshape(PAIRS, P, 2 * D)

    def chunked(v):
        return v.reshape(KC, P, v.shape[-1]).transpose(1, 0, 2)

    consts, halves = shape_constants()
    freqs = a["L0_attn_freqs"]
    arrays = {
        "x": rows(a["x"]), "xT": columns(a["x"]),
        "ctxt": rows(a["ctx_1024"]), "ctxT": columns(a["ctx_1024"]),
        "wvT": chunked(a["L0_attn_Wv"].T), "woT": chunked(a["L0_attn_Wo"].T),
        "freq": _np.concatenate([_np.broadcast_to(freqs, (P, D)), freqs.reshape(KC, P).T,
                                 _np.arange(P, dtype=freqs.dtype)[:, None]], axis=1),
        "routerT": chunked(a["L0_ffn_router_w"].T),
        "weights": _np.concatenate([
            a["L0_ffn_up_proj"].reshape(E, KC, P, 2 * DH).transpose(0, 2, 1, 3).reshape(E, P, W_DOWN),
            a["L0_ffn_down_proj"].reshape(E, KC, P, D).transpose(0, 2, 1, 3).reshape(E, P, KC * D)], axis=2),
        "consts": consts, "halves": halves,
    }
    arrays = {k: _np.ascontiguousarray(v) for k, v in arrays.items()}
    nc = _bacc.Bacc("TRN2", target_bir_lowering=False, num_devices=1)
    args = {k: nc.dram_tensor(f"in_{k}", v.shape, _mybir.dt.from_np(v.dtype), kind="ExternalInput").ap()
            for k, v in arrays.items()}
    out = nc.dram_tensor("out_0", (PAIRS, P, 2 * D), _mybir.dt.float32, kind="ExternalOutput").ap()
    decoder_block(nc, out=out, **args)
    r = _run(nc, [{f"in_{k}": v for k, v in arrays.items()}], core_ids=[0])
    got = r.results[0]["out_0"]
    return got.reshape(PAIRS, P, 2, D).transpose(0, 2, 1, 3).reshape(B, T, D)
```
